# Optimizing a Trainium2 kernel written in Bass

```python
import numpy as np
import jax
import jax.numpy as jnp

def _softmax(x, axis=-1):
    return jax.nn.softmax(x, axis=axis)

def _gelu(x):
    return jax.nn.gelu(x, approximate=True)

def _silu(x):
    return jax.nn.silu(x)

def _sigmoid(x):
    return jax.nn.sigmoid(x)

def _layernorm(x, axis=-1, eps=1e-05):
    m = jnp.mean(x, axis=axis, keepdims=True)
    v = jnp.var(x, axis=axis, keepdims=True)
    return (x - m) / jnp.sqrt(v + eps)

def _scatter_add(tgt, idx, src, axis=0):
    return tgt.at[idx].add(src)

def _segment_sum(src, seg, n):
    return jax.ops.segment_sum(src, seg, n)
kernel_name = 'mk_decoder_postln_d1_seqx_r8_25d5a0'

def setup_inputs(seed: int=0):
    np.random.seed(seed)
    _w = jnp.asarray

    def _rec_inputs():
        import jax
        import jax.numpy as jnp
        _rk = jax.random.key(seed)
        x = 7.22e-05 + 1 * jax.random.normal(jax.random.fold_in(_rk, 1), (32, 128, 128), jnp.float32)
        _lenS = 128 - jax.random.randint(jax.random.fold_in(_rk, 7), (32,), 0, max(1, 128 // 4) + 1, jnp.int32)
        _lenS2 = 128 - jax.random.randint(jax.random.fold_in(_rk, 8), (32,), 0, max(1, 128 // 4) + 1, jnp.int32)
        _ctx_1024P = jax.random.normal(jax.random.fold_in(_rk, 11), (32, 16, 128), jnp.float32)
        _ctx_1024c = jax.random.dirichlet(jax.random.fold_in(_rk, 511), 0.3 * jnp.ones((16,), jnp.float32), (32, 128))
        _ctx_1024t = jnp.einsum('bsk,bkd->bsd', _ctx_1024c, _ctx_1024P)
        _ctx_1024t = _ctx_1024t * jax.lax.rsqrt(jnp.mean(jnp.square(_ctx_1024t)) + 1e-12) * 0.953939
        ctx_1024 = 4.13588e-05 + 0.999923 * (_ctx_1024t + 0.3 * jax.random.normal(jax.random.fold_in(_rk, 611), (32, 128, 128), jnp.float32))
        return (x, ctx_1024)
    x, ctx_1024 = _rec_inputs()

    def _L0_attn_setup():
        import jax, jax.numpy as jnp
        import numpy as np
        NUM_LANDMARKS = 64
        key = jax.random.key(seed)
        ks = jax.random.split(key, 4)
        B, S, D = (4, 512, 128)
        init = 0.02
        return {'hidden_states': jax.random.normal(ks[0], (B, S, D), dtype=jnp.float32), 'Wq': jax.random.normal(ks[1], (D, D), dtype=jnp.float32) * init, 'bq': jnp.zeros((D,), dtype=jnp.float32), 'Wk': jax.random.normal(ks[2], (D, D), dtype=jnp.float32) * init, 'bk': jnp.zeros((D,), dtype=jnp.float32), 'Wv': jax.random.normal(ks[3], (D, D), dtype=jnp.float32) * init, 'bv': jnp.zeros((D,), dtype=jnp.float32)}
    _L0_attn_all = _L0_attn_setup()
    _L0_attn_in = {k: v for k, v in _L0_attn_all.items() if k in ('Wq', 'bq', 'Wk', 'bk', 'Wv', 'bv')}
    del _L0_attn_all

    def _L0_xattn_setup():
        import jax, jax.numpy as jnp
        import numpy as np
        D_MODEL = 128
        N_HEADS = 16
        HEAD_DIM = D_MODEL // N_HEADS
        key = jax.random.key(seed)
        ks = jax.random.split(key, 6)
        B, S = (4, 256)
        query = jax.random.normal(ks[0], (B, S, D_MODEL), dtype=jnp.float32)
        key_value = jax.random.normal(ks[1], (B, S, D_MODEL), dtype=jnp.float32)
        scale = 1.0 / np.sqrt(D_MODEL)
        Wq = jax.random.normal(ks[2], (D_MODEL, D_MODEL), dtype=jnp.float32) * scale
        Wk = jax.random.normal(ks[3], (D_MODEL, D_MODEL), dtype=jnp.float32) * scale
        Wv = jax.random.normal(ks[4], (D_MODEL, D_MODEL), dtype=jnp.float32) * scale
        Wo = jax.random.normal(ks[5], (D_MODEL, D_MODEL), dtype=jnp.float32) * scale
        return {'query': query, 'key_value': key_value, 'Wq': Wq, 'Wk': Wk, 'Wv': Wv, 'Wo': Wo}
    _L0_xattn_all = _L0_xattn_setup()
    _L0_xattn_in = {k: v for k, v in _L0_xattn_all.items() if k in ('Wq', 'Wk', 'Wv', 'Wo')}
    del _L0_xattn_all

    def _L0_ffn_setup():
        import jax, jax.numpy as jnp
        import numpy as np
        B, S, D, H, O, E, K = (4, 256, 128, 256, 128, 8, 2)
        key = jax.random.key(seed)
        ks = jax.random.split(key, 8)
        x = jax.random.normal(ks[0], (B, S, D), dtype=jnp.float32)
        gate_w = jax.random.uniform(ks[1], (E, D), dtype=jnp.float32, minval=-1, maxval=1) * np.sqrt(6.0 / D)
        gate_b = jnp.zeros((E,), dtype=jnp.float32)
        w1 = jax.random.uniform(ks[2], (E, D, H), dtype=jnp.float32, minval=-1, maxval=1) * np.sqrt(6.0 / D)
        b1 = jnp.zeros((E, H), dtype=jnp.float32)
        w2 = jax.random.uniform(ks[3], (E, H, O), dtype=jnp.float32, minval=-1, maxval=1) * np.sqrt(6.0 / H)
        b2 = jnp.zeros((E, O), dtype=jnp.float32)
        return {'x': x, 'gate_w': gate_w, 'gate_b': gate_b, 'w1': w1, 'b1': b1, 'w2': w2, 'b2': b2}
    _L0_ffn_all = _L0_ffn_setup()
    _L0_ffn_in = {k: v for k, v in _L0_ffn_all.items() if k in ('gate_w', 'gate_b', 'w1', 'b1', 'w2', 'b2')}
    del _L0_ffn_all
    return {'x': x, 'ctx_1024': ctx_1024, 'L0_attn_Wq': _L0_attn_in['Wq'], 'L0_attn_bq': _L0_attn_in['bq'], 'L0_attn_Wk': _L0_attn_in['Wk'], 'L0_attn_bk': _L0_attn_in['bk'], 'L0_attn_Wv': _L0_attn_in['Wv'], 'L0_attn_bv': _L0_attn_in['bv'], 'L0_xattn_Wq': _L0_xattn_in['Wq'], 'L0_xattn_Wk': _L0_xattn_in['Wk'], 'L0_xattn_Wv': _L0_xattn_in['Wv'], 'L0_xattn_Wo': _L0_xattn_in['Wo'], 'L0_ffn_gate_w': _L0_ffn_in['gate_w'], 'L0_ffn_gate_b': _L0_ffn_in['gate_b'], 'L0_ffn_w1': _L0_ffn_in['w1'], 'L0_ffn_b1': _L0_ffn_in['b1'], 'L0_ffn_w2': _L0_ffn_in['w2'], 'L0_ffn_b2': _L0_ffn_in['b2']}

def reference(x, ctx_1024, L0_attn_Wq, L0_attn_bq, L0_attn_Wk, L0_attn_bk, L0_attn_Wv, L0_attn_bv, L0_xattn_Wq, L0_xattn_Wk, L0_xattn_Wv, L0_xattn_Wo, L0_ffn_gate_w, L0_ffn_gate_b, L0_ffn_w1, L0_ffn_b1, L0_ffn_w2, L0_ffn_b2):
    import jax
    import jax.numpy as jnp

    def _L0_attn_ref(hidden_states, Wq, bq, Wk, bk, Wv, bv):
        import jax, jax.numpy as jnp
        import numpy as np
        NUM_LANDMARKS = 64
        B, S, D = hidden_states.shape
        L = NUM_LANDMARKS
        q = hidden_states @ Wq + bq
        k = hidden_states @ Wk + bk
        v = hidden_states @ Wv + bv
        q = jax.nn.softmax(q, axis=-1)
        k = jax.nn.softmax(k, axis=-1)
        k_landmarks = k.reshape(B, L, S // L, D).mean(axis=2)
        kernel_1 = jnp.einsum('bqd,bkd->bqk', q, k_landmarks)
        kernel_2 = jnp.einsum('bkd,bld->bkl', k_landmarks, k)
        kernel_3 = k * v
        mid = jnp.einsum('bkl,bld->bkd', kernel_2, kernel_3)
        output = jnp.einsum('bqk,bkd->bqd', kernel_1, mid)
        return output

    def _L0_xattn_ref(query, key_value, Wq, Wk, Wv, Wo):
        import jax, jax.numpy as jnp
        import numpy as np
        D_MODEL = 128
        N_HEADS = 16
        HEAD_DIM = D_MODEL // N_HEADS
        B, S, _ = query.shape
        H, Dh = (N_HEADS, HEAD_DIM)
        q = (query @ Wq.T).reshape(B, S, H, Dh).transpose(0, 2, 1, 3)
        k = (key_value @ Wk.T).reshape(B, S, H, Dh).transpose(0, 2, 1, 3)
        v = (key_value @ Wv.T).reshape(B, S, H, Dh).transpose(0, 2, 1, 3)
        scale = Dh ** (-0.5)
        scores = jnp.einsum('bhqd,bhkd->bhqk', q, k) * scale
        causal = jnp.tril(jnp.ones((S, S), dtype=bool))
        scores = jnp.where(causal, scores, -jnp.inf)
        attn = jax.nn.softmax(scores, axis=-1)
        out = jnp.einsum('bhqk,bhkd->bhqd', attn, v)
        out = out.transpose(0, 2, 1, 3).reshape(B, S, H * Dh)
        return out @ Wo.T

    def _L0_ffn_ref(x, gate_w, gate_b, w1, b1, w2, b2):
        import jax, jax.numpy as jnp
        import numpy as np
        B, S, D, H, O, E, K = (4, 256, 128, 256, 128, 8, 2)
        logits = jnp.einsum('bsd,ed->bse', x, gate_w) + gate_b
        probs = jax.nn.softmax(logits, axis=-1)
        topk_vals, topk_idx = jax.lax.top_k(probs, K)
        h = jax.nn.relu(jnp.einsum('bsd,edh->bseh', x, w1) + b1)
        expert_out = jnp.einsum('bseh,eho->bseo', h, w2) + b2
        sel = jnp.take_along_axis(expert_out, topk_idx[..., None], axis=2)
        return jnp.sum(sel * topk_vals[..., None], axis=2)
    x = _layernorm(x + _L0_attn_ref(x, L0_attn_Wq, L0_attn_bq, L0_attn_Wk, L0_attn_bk, L0_attn_Wv, L0_attn_bv), axis=-1)
    x = _layernorm(x + _L0_xattn_ref(x, ctx_1024, L0_xattn_Wq, L0_xattn_Wk, L0_xattn_Wv, L0_xattn_Wo), axis=-1)
    x = _layernorm(x + _L0_ffn_ref(x, L0_ffn_gate_w, L0_ffn_gate_b, L0_ffn_w1, L0_ffn_b1, L0_ffn_w2, L0_ffn_b2), axis=-1)
    return x

_drawn_inputs = setup_inputs


def setup_inputs(seed=0):
    import zlib

    import numpy as np

    out = dict(_drawn_inputs(seed))
    spreads = {'L0_attn_bq': (0.0, 2.0),
     'L0_attn_bk': (0.0, 2.0),
     'L0_attn_bv': (0.0, 0.8),
     'L0_ffn_gate_b': (0.0, 0.1),
     'L0_ffn_b1': (0.0, 0.1),
     'L0_ffn_b2': (0.0, 0.1)}
    factors = {'L0_attn_Wq': 25.324, 'L0_attn_Wk': 8.0, 'L0_attn_Wv': 8.0}
    for name, (base, spread) in spreads.items():
        noise = np.random.default_rng([zlib.crc32(name.encode()), seed]).standard_normal(out[name].shape)
        drawn = base * np.exp(spread * noise) if base else spread * noise
        out[name] = jnp.asarray(drawn.astype(out[name].dtype))
    for name, factor in factors.items():
        out[name] = (out[name] * factor).astype(out[name].dtype)
    return out
```

```python
import concourse.bass as bass
from concourse import mybir
from contextlib import ExitStack

F32 = mybir.dt.float32
BF16 = mybir.dt.bfloat16
ALU = mybir.AluOpType
ACT = mybir.ActivationFunctionType
AX = mybir.AxisListType.X

P = 128
EPS = 1e-5
MASKED = -1e30
LOWEST = -3e38


def decoder_layer(nc, x, x_t, ctx_t, w_qkv, b_qkv, xwq_t, xwk_t, xwv_t, xwo_t, gate_t, gate_b, w1, b1, w2, b2, out):
    NB, S, D = x.shape
    E, _, HID = w1.shape
    GB = 2
    T = GB * S
    NG = NB // GB
    NH, DH = 16, 8
    NJ = NH // 2
    QUADS = NH // 4
    UNITS = GB * QUADS
    SCALE = float(DH) ** -0.5
    NHB = HID // P
    K_OUT = 32
    Q_PART = [0, 0, 0, 1, 1, 2]
    K_PART = [0, 1, 2, 0, 1, 0]
    TERMS = len(Q_PART)
    M_ROW = TERMS * DH
    assert D == P and S == P and NHB == 2 and M_ROW + 3 <= 64

    with ExitStack() as ctx:
        def sb(name, shape, dt=F32):
            return ctx.enter_context(nc.sbuf_tensor(name, shape, dt))

        def sem(name):
            return ctx.enter_context(nc.semaphore(name))

        ident = sb("ident", [P, P])
        ident_b = sb("ident_b", [P, P], BF16)
        ones_b = sb("ones_b", [P, P], BF16)
        pairs = sb("pairs", [P, P])
        mask4 = sb("mask4", [P, 4, S], BF16)
        m_ones = sb("m_ones", [P, 1], BF16)
        m_tmp = sb("m_tmp", [P, 2], BF16)
        zero_rows = sb("zero_rows", [P, NJ * T], BF16)
        wqkv_s = sb("wqkv_s", [P, 3 * D])
        bias_bc = sb("bias_bc", [P, 3 * D])
        bias_p = sb("bias_p", [P, 3, 3 * D], BF16)
        bias_r = sb("bias_r", [P, 3 * D])
        bias_m = sb("bias_m", [P, 3, 3 * D], BF16)
        xwq_s = sb("xwq_s", [P, D])
        xwk_s = sb("xwk_s", [P, D])
        xwv_s = sb("xwv_s", [P, D])
        xwo_s = sb("xwo_s", [P, D])
        gate_s = sb("gate_s", [P, P])
        gateb_s = sb("gateb_s", [P, E])
        w1_s = sb("w1_s", [P, E, HID])
        b1_s = sb("b1_s", [P, E, NHB])
        w2_s = sb("w2_s", [P, E, NHB, D])
        b2_s = sb("b2_s", [P, D])
        x_s = sb("x_s", [P, GB, D])
        xT_s = sb("xT_s", [P, T])
        cT_s = sb("cT_s", [P, T])
        nmax1 = sb("nmax1", [P, GB, 2])
        eqk = sb("eqk", [P, GB, 2, D])
        sum1 = sb("sum1", [P, GB, 2])
        rs1 = sb("rs1", [P, GB, 2])
        kn = sb("kn", [P, GB, D])
        mkkv = sb("mkkv", [P, GB, 2, D])
        eqT = sb("eqT", [P, T])
        gh = sb("gh", [P, GB, 2, D])
        r_s = sb("r_s", [P, GB, D])
        r1 = sb("r1", [P, GB, D])
        st1 = sb("st1", [P, GB, 6])
        mv1 = sb("mv1", [P, GB, 2])
        rstd1 = sb("rstd1", [P, GB])
        x1 = sb("x1", [P, GB, D])
        eps_s = sb("eps_s", [P, GB])
        mhalf = sb("mhalf", [P, GB])
        veps = sb("veps", [P, 3, GB])
        x1T = sb("x1T", [P, T])
        vaug = sb("vaug", [P, GB, NH, K_OUT])
        parts = sb("parts", [P, 3, 2, T], BF16)
        rest = sb("rest", [P, 2 * T])
        rest2 = sb("rest2", [P, 2 * T])
        q_zb = sb("q_zb", [P, 2, NJ, GB, S], BF16)
        k_dn = sb("k_dn", [P, NJ, GB, S], BF16)
        nm = sb("nm", [P, 2, NJ, GB])
        m_p = sb("m_p", [NH * GB, 3, S], BF16)
        m_r = sb("m_r", [NH * GB, 2, S])
        at = sb("at", [P, 3, 4, S])
        oT = sb("oT", [P, GB, QUADS, S])
        rden = sb("rden", [P, GB, NH])
        on = sb("on", [P, GB, D])
        onT = sb("onT", [P, GB, S])
        r2 = sb("r2", [P, GB, D])
        st2 = sb("st2", [P, GB, 6])
        mv2 = sb("mv2", [P, GB, 2])
        rstd2 = sb("rstd2", [P, GB])
        x2 = sb("x2", [P, GB, D])
        x2T = sb("x2T", [P, T])
        lg = sb("lg", [P, GB, 2 * E])
        top = sb("top", [P, GB, 8])
        two = sb("two", [P, GB, 8])
        rep = sb("rep", [P, GB, 2 * E])
        chosen = sb("chosen", [P, GB, E])
        lsh = sb("lsh", [P, GB, E])
        eg = sb("eg", [P, GB, E])
        gsum = sb("gsum", [P, GB])
        grec = sb("grec", [P, GB])
        gmul = sb("gmul", [P, GB, E])
        gates = sb("gates", [P, GB, P])
        gT = sb("gT", [P, GB, S])
        hs = sb("hs", [P, 2, NHB, T])
        acc = sb("acc", [P, GB, D])
        st3 = sb("st3", [P, GB, 6])
        mv3 = sb("mv3", [P, GB, 2])
        rstd3 = sb("rstd3", [P, GB])
        o_s = sb("o_s", [P, GB, D])

        W = [ctx.enter_context(nc.psum_tensor(f"W{n}", [P, 512], F32)) for n in range(5)]
        HB = [ctx.enter_context(nc.psum_tensor(f"HB{n}", [P, 512], F32)) for n in range(2)]
        YB = ctx.enter_context(nc.psum_tensor("YB", [P, 512], F32))
        S_BANK = [W[0], W[1], W[3]]
        ST_BANK = [W[0], W[1], W[4]]

        const_step = sem("const_step")
        consts_ready = sem("consts_ready")
        bias_in, bias_step, bias_ready = sem("bias_in"), sem("bias_step"), sem("bias_ready")
        attn_w_in, xattn_w_in, expert_w_in = sem("attn_w_in"), sem("xattn_w_in"), sem("expert_w_in")
        dve_set = sem("dve_set")
        x_in, xT_in, cT_in = sem("x_in"), sem("xT_in"), sem("cT_in")
        zeros_in, q_in, k_in, m_in, gateb_in_stores = sem("zeros_in"), sem("q_in"), sem("k_in"), sem("m_in"), sem("gateb_in_stores")
        qkv_ps, mk_ps, eqT_ps, gh_ps, r_ps, attn_ps = (sem(n) for n in ("qkv_ps", "mk_ps", "eqT_ps", "gh_ps", "r_ps", "attn_ps"))
        x1T_ps, kp_ps, qp_ps, v_ps = (sem(n) for n in ("x1T_ps", "kp_ps", "qp_ps", "v_ps"))
        s_ps, mT_ps, st_ps, av_ps, oo_ps, onT_ps, y_ps = (sem(n) for n in ("s_ps", "mT_ps", "st_ps", "av_ps", "oo_ps", "onT_ps", "y_ps"))
        x2T_ps, lg_ps, gT_ps, b2_ps, h_ps, ye_ps = (sem(n) for n in ("x2T_ps", "lg_ps", "gT_ps", "b2_ps", "h_ps", "ye_ps"))
        e_done, mk_done, eqT_done, r_done, x1T_done = (sem(n) for n in ("e_done", "mk_done", "eqT_done", "r_done", "x1T_done"))
        p1_done, p2_done, exp_done, oT_done, onT_done = (sem(n) for n in ("p1_done", "p2_done", "exp_done", "oT_done", "onT_done"))
        x2T_done, eg_done, gT_done, h0_done = (sem(n) for n in ("x2T_done", "eg_done", "gT_done", "h0_done"))
        nmax_done, rs1_done, kn_done, kv_done, gh_done = (sem(n) for n in ("nmax_done", "rs1_done", "kn_done", "kv_done", "gh_done"))
        r1_done, st1_done, mv1_done, rstd1_done, x1_done = (sem(n) for n in ("r1_done", "st1_done", "mv1_done", "rstd1_done", "x1_done"))
        vaug_done, rest_done, rest2_done, p3_done, nm_done = (sem(n) for n in ("vaug_done", "rest_done", "rest2_done", "p3_done", "nm_done"))
        mp_step = sem("mp_step")
        rden_done, on_done = sem("rden_done"), sem("on_done")
        r2_done, st2_done, mv2_done, rstd2_done, x2_done = (sem(n) for n in ("r2_done", "st2_done", "mv2_done", "rstd2_done", "x2_done"))
        gate2 = sem("gate2")
        lg_done, gate_step, gates_done, acc0_done = (sem(n) for n in ("lg_done", "gate_step", "gates_done", "acc0_done"))
        h1_done, acc_done = sem("h1_done"), sem("acc_done")
        st3_done, mv3_done, rstd3_done, o_done = (sem(n) for n in ("st3_done", "mv3_done", "rstd3_done", "o_done"))
        sel_done = sem("sel_done")
        veps_done = [sem(f"veps{n}_done") for n in (1, 2, 3)]

        def wait(eng, s, value):
            if not (isinstance(value, int) and value <= 0):
                eng.wait_ge(s, value)

        def hold(eng, s, value):
            at_least = value if isinstance(value, int) else eng.snap(eng.to_reg(value))
            eng.wait_ge(consts_ready, 1)
            eng.wait_ge(s, at_least)

        def each_group(eng, attention, experts):
            attention(0, None)
            with eng.Fori(1, NG) as i:
                attention(i, experts)
            for e in range(E + 1):
                experts(NG, e)

        block = ctx.enter_context(nc.Block())

        @block.sync
        def _(sp):
            sp.dma_start(wqkv_s[:, :].rearrange("p (w n) -> p w n", w=3), w_qkv.rearrange("w p n -> p w n")).then_inc(attn_w_in, 16)

            def loads(i):
                wait(sp, qkv_ps, i * GB)
                sp.dma_start(xT_s[:, :], x_t[:, bass.ds(i * T, T)]).then_inc(xT_in, 16)
                wait(sp, v_ps, i)
                wait(sp, kp_ps, i)
                sp.dma_start(cT_s[:, :], ctx_t[:, bass.ds(i * T, T)]).then_inc(cT_in, 16)
                wait(sp, r1_done, i * GB)
                sp.dma_start(x_s[:, :, :], x[bass.ds(i * GB, GB), :, :].rearrange("b s d -> s b d")).then_inc(x_in, 16)

            def stacks(i):
                wait(sp, st_ps, i * UNITS)
                for par in range(2):
                    rows = 64 * par + M_ROW
                    sp.dma_start(q_zb[rows:rows + 3, par, :, :, :].rearrange("p j b s -> p (j b s)"), zero_rows[0:3, :]).then_inc(zeros_in, 16)
                for qk, part_of, done in ((1, K_PART, k_in), (0, Q_PART, q_in)):
                    for part in range(3):
                        if part == 0:
                            sp.wait_ge(p1_done, i + 1)
                        elif part == 1:
                            sp.wait_ge(p2_done, i + 1)
                        else:
                            sp.wait_ge(p3_done, i + 1)
                        for t in range(TERMS):
                            if part_of[t] != part:
                                continue
                            for par in range(2):
                                rows = slice(64 * par + DH * t, 64 * par + DH * t + DH)
                                dst = k_dn[rows, :, :, :] if qk else q_zb[rows, par, :, :, :]
                                sp.dma_start(dst.rearrange("d j b s -> d j (b s)"), parts[64 * par:64 * par + 64, part, qk, :]).then_inc(done, 16)

            def attention(i, experts):
                loads(i)
                if isinstance(i, int):
                    sp.dma_start(xwk_s[:, :], xwk_t).then_inc(xattn_w_in, 16)
                    sp.dma_start(xwv_s[:, :], xwv_t).then_inc(xattn_w_in, 16)
                    sp.dma_start(xwq_s[:, :], xwq_t).then_inc(xattn_w_in, 16)
                    sp.dma_start(xwo_s[:, :], xwo_t).then_inc(xattn_w_in, 16)
                    sp.wait_ge(dve_set, 4)
                    sp.dma_start(gate_s[:, 0:E], gate_t).then_inc(expert_w_in, 16)
                    sp.dma_start(b2_s[0:E, :], b2).then_inc(expert_w_in, 16)
                    sp.dma_start(w1_s[:, :, :], w1.rearrange("e d h -> d e h")).then_inc(expert_w_in, 16)
                    sp.dma_start(b1_s[:, :, :], b1).then_inc(expert_w_in, 16)
                    sp.dma_start(w2_s[:, :, :, :], w2.rearrange("e (n p) o -> p e n o", p=P)).then_inc(expert_w_in, 16)
                    sp.wait_ge(consts_ready, 1)
                stacks(i)
                sp.wait_ge(mp_step, 4 * (i + 1))
                for par in range(2):
                    for part in range(3):
                        row = 64 * par + M_ROW + part
                        sp.dma_start(q_zb[row:row + 1, par, :, :, :].rearrange("o j b s -> o (j b) s"),
                                     m_p[NJ * GB * par:NJ * GB * (par + 1), part, :]).then_inc(m_in, 16)

            attention(0, None)
            with sp.Fori(1, NG) as i:
                attention(i, None)

        N_FILLS = 9
        K_DMAS = Q_DMAS = TERMS * 2
        M_DMAS = 3 * 2

        @block.gpsimd
        def _(pool):
            pool.dma_start(bias_bc[:, :], b_qkv.rearrange("(o n) -> o n", o=1).broadcast_to([P, 3 * D])).then_inc(bias_in, 16)
            pool.dma_start(gateb_s[:, :], gate_b.rearrange("(o n) -> o n", o=1).broadcast_to([P, E])).then_inc(gateb_in_stores, 16)
            pool.memset(ident[:, :], 0.0).then_inc(const_step, 1)
            pool.memset(ident_b[:, :], 0.0).then_inc(const_step, 1)
            pool.memset(pairs[:, :], 0.25).then_inc(const_step, 1)
            pool.memset(mask4[:, :, :], 0.0).then_inc(const_step, 1)
            pool.memset(m_tmp[:, :], 1.0).then_inc(const_step, 1)
            pool.memset(eps_s[:, :], EPS).then_inc(const_step, 1)
            pool.memset(mhalf[:, :], -0.5).then_inc(const_step, 1)
            pool.wait_ge(const_step, 7)
            for m in (ident, ident_b):
                pool.affine_select(out=m[:, :], in_=m[:, :], compare_op=ALU.not_equal, fill=1.0, base=0,
                                   pattern=[[-1, P]], channel_multiplier=1).then_inc(const_step, 1)
            pv = pairs[:, :].rearrange("p (j w) -> p j w", w=2)
            pool.affine_select(out=pv, in_=pv, compare_op=ALU.is_ge, fill=0.0, base=0,
                               pattern=[[-2, P // 2], [0, 2]], channel_multiplier=1).then_inc(const_step, 1)
            pool.affine_select(out=mask4[:, :, :], in_=mask4[:, :, :], compare_op=ALU.is_ge, fill=MASKED, base=0,
                               pattern=[[0, 4], [-1, S]], channel_multiplier=1).then_inc(const_step, 1)
            pool.affine_select(out=m_tmp[:, :], in_=m_tmp[:, :], compare_op=ALU.is_ge, fill=0.0,
                               base=-M_ROW, pattern=[[-64, 2]], channel_multiplier=1).then_inc(const_step, 1)
            pool.wait_ge(const_step, 12)
            pool.affine_select(out=pv, in_=pv, compare_op=ALU.is_ge, fill=0.0, base=1,
                               pattern=[[2, P // 2], [0, 2]], channel_multiplier=-1).then_inc(const_step, 1)
            pool.affine_select(out=m_tmp[:, :], in_=m_tmp[:, :], compare_op=ALU.is_ge, fill=0.0,
                               base=M_ROW + 2, pattern=[[64, 2]], channel_multiplier=-1).then_inc(const_step, 1)

            def inverse_deviation(i, n, mv, mv_done, rstd, rstd_done):
                pool.wait_ge(mv_done, i + 1)
                pool.tensor_tensor(veps[:, n, :], mv[:, :, 1], eps_s[:, :], ALU.add).then_inc(veps_done[n], 1)
                pool.wait_ge(veps_done[n], i + 1)
                pool.tensor_tensor(rstd[:, :], veps[:, n, :], mhalf[:, :], ALU.pow).then_inc(rstd_done, 1)

            def attention(i, experts):
                inverse_deviation(i, 0, mv1, mv1_done, rstd1, rstd1_done)
                if experts:
                    experts(i, None)
                for u in range(UNITS):
                    hold(pool, exp_done, UNITS * i + u + 1)
                    pool.affine_select(out=at[:, u % 3, :, :], in_=at[:, u % 3, :, :], compare_op=ALU.is_ge, fill=0.0,
                                       base=0, pattern=[[0, 4], [1, S]], channel_multiplier=-1).then_inc(sel_done, 1)
                inverse_deviation(i, 1, mv2, mv2_done, rstd2, rstd2_done)

            def experts(i, e):
                if e is None or e == E:
                    inverse_deviation(i - 1, 2, mv3, mv3_done, rstd3, rstd3_done)
                    hold(pool, o_done, GB * i)
                    pool.dma_start(out[bass.ds(i * GB - GB, GB), :, :].rearrange("b s d -> s b d"), o_s[:, :, :]).then_inc(gateb_in_stores, 16)

            each_group(pool, attention, experts)
            pool.wait_ge(gateb_in_stores, 16 * (NG + 1))

        @block.scalar
        def _(act):
            def experts(i, e):
                if e < E:
                    act.wait_ge(h_ps, E * i - E + e + 1)
                    act.activation(hs[:, e % 2, 0, :], HB[e % 2][:, 0:T], ACT.Relu, bias=b1_s[:, e, 0:1]).then_inc(h0_done, 1)

            def attention(i, experts):
                if experts:
                    experts(i, 0)
                for b in range(GB):
                    for n in range(2):
                        act.wait_ge(nmax_done, GB * i + b + 1)
                        if b == 0 and n == 0:
                            wait(act, eqT_ps, i)
                            wait(act, r1_done, GB * i)
                        act.activation(eqk[:, b, n, :], W[b][:, n * D:n * D + D], ACT.Exp, bias=nmax1[:, b, n:n + 1],
                                       accum_out=sum1[:, b, n:n + 1]).then_inc(e_done, 1)
                if experts:
                    experts(i, 1)
                act.wait_ge(eqT_ps, i + 1)
                act.activation(eqT[:, :], W[3][:, 0:T], ACT.Copy).then_inc(eqT_done, 1)
                act.wait_ge(mk_ps, i + 1)
                act.activation(mkkv[:, :, 0, :], W[2][:, T:2 * T].rearrange("p (b d) -> p b d", b=GB), ACT.Copy).then_inc(mk_done, 1)
                if experts:
                    experts(i, 2)
                    experts(i, 3)
                act.wait_ge(r_ps, i + 1)
                act.activation(r_s[:, :, :], W[1][:, 0:T].rearrange("p (b d) -> p b d", b=GB), ACT.Copy).then_inc(r_done, 1)
                if experts:
                    experts(i, 4)
                act.wait_ge(x1T_ps, i + 1)
                act.activation(x1T[:, :], W[2][:, 0:T], ACT.Copy).then_inc(x1T_done, 1)
                act.wait_ge(kp_ps, i + 1)
                act.wait_ge(qp_ps, i + 1)
                wait(act, q_in, 16 * Q_DMAS * i)
                act.activation(parts[:, 0, :, :], W[4][:, :].rearrange("p (n t) -> p n t", n=2), ACT.Copy).then_inc(p1_done, 1)
                if experts:
                    experts(i, 5)
                act.wait_ge(rest_done, i + 1)
                act.activation(parts[:, 1, :, :], rest[:, :].rearrange("p (n t) -> p n t", n=2), ACT.Copy).then_inc(p2_done, 1)
                if experts:
                    experts(i, 6)
                    experts(i, 7)
                for u in range(UNITS):
                    b = u // QUADS
                    act.wait_ge(st_ps, UNITS * i + u + 1)
                    wait(act, av_ps, UNITS * i + u - 2)
                    act.activation(at[:, u % 3, :, :], ST_BANK[u % 3][:, :].rearrange("p (h s) -> p h s", h=4),
                                   ACT.Exp, scale=SCALE).then_inc(exp_done, 1)
                    if u == 6:
                        attn_out(i, 0)
                attn_out(i, 1)
                for b in range(GB):
                    act.wait_ge(onT_ps, GB * i + b + 1)
                    act.activation(onT[:, b, :], W[2 + b][:, 0:S], ACT.Copy).then_inc(onT_done, 1)
                act.wait_ge(x2T_ps, i + 1)
                act.activation(x2T[:, :], W[0][:, 0:T], ACT.Copy).then_inc(x2T_done, 1)
                act.wait_ge(gate_step, 7 * i + 6)
                act.activation(eg[:, :, :], lsh[:, :, :], ACT.Exp).then_inc(eg_done, 1)
                act.wait_ge(gT_ps, i + 1)
                act.activation(gT[:, :, :], W[0][:, T:2 * T].rearrange("p (b s) -> p b s", b=GB), ACT.Copy).then_inc(gT_done, 1)

            def attn_out(i, b):
                act.wait_ge(av_ps, UNITS * i + QUADS * (b + 1))
                act.activation(oT[:, b, :, :], W[2 + b][:, :].rearrange("p (c s) -> p c s", c=QUADS), ACT.Copy).then_inc(oT_done, 1)

            act.wait_ge(consts_ready, 1)
            attention(0, None)
            with act.Fori(1, NG) as i:
                attention(i, experts)
            for e in range(E):
                experts(NG, e)

        @block.tensor
        def _(pe):
            mm = nc.tensor.matmul

            def hidden(i, e):
                if e == 0:
                    pe.wait_ge(x2T_done, i)
                if e >= 2:
                    pe.wait_ge(h0_done, E * i - E + e - 1)
                    pe.wait_ge(h1_done, E * i - E + e - 1)
                for n in range(NHB):
                    last = mm(HB[e % 2][:, n * T:n * T + T], w1_s[:, e, n * P:n * P + P], x2T[:, :], start=True, stop=True)
                last.then_inc(h_ps, 1)

            def expert_out(i, e):
                pe.wait_ge(h0_done, E * i - E + e + 1)
                pe.wait_ge(h1_done, E * i - E + e + 1)
                if e == 0:
                    pe.wait_ge(acc0_done, i)
                else:
                    pe.wait_ge(acc_done, GB * (E * i - E + e))
                for b in range(GB):
                    for n in range(NHB):
                        last = mm(YB[:, b * D:b * D + D], hs[:, e % 2, n, b * S:b * S + S], w2_s[:, e, n, :],
                                  start=(n == 0), stop=(n == NHB - 1))
                last.then_inc(ye_ps, 1)

            def experts(i, step):
                if step == 0:
                    hidden(i, 0)
                if step < E - 1:
                    hidden(i, step + 1)
                if step < E:
                    expert_out(i, step)

            def attention(i, experts):
                pe.wait_ge(xT_in, 16 * (i + 1))
                if experts is None:
                    pe.wait_ge(attn_w_in, 16)
                    pe.wait_ge(bias_ready, 1)
                    pe.wait_ge(consts_ready, 1)
                wait(pe, gT_done, i)
                wait(pe, acc0_done, i)
                for b in range(GB):
                    mm(W[b][:, 0:3 * D], xT_s[:, b * S:b * S + S], wqkv_s[:, :], start=True, stop=False)
                    for part in range(3):
                        last = mm(W[b][:, 0:3 * D], ones_b[:, :], bias_m[:, part, :], start=False, stop=(part == 2))
                    last.then_inc(qkv_ps, 1)
                if experts is None:
                    pe.wait_ge(xattn_w_in, 64)
                pe.wait_ge(cT_in, 16 * (i + 1))
                wait(pe, exp_done, UNITS * i)
                mm(W[4][:, T:2 * T], xwk_s[:, :], cT_s[:, :], start=True, stop=True).then_inc(kp_ps, 1)
                wait(pe, r2_done, GB * i)
                for b in range(GB):
                    last = mm(W[2][:, b * D:b * D + D], cT_s[:, b * S:b * S + S], xwv_s[:, :], start=True, stop=True)
                last.then_inc(v_ps, 1)
                if experts:
                    experts(i, 0)
                pe.wait_ge(e_done, 2 * GB * (i + 1))
                for b in range(GB):
                    last = nc.tensor.transpose(W[3][:, b * S:b * S + S], eqk[:, b, 0, :], ident[:, :])
                last.then_inc(eqT_ps, 1)
                pe.wait_ge(kn_done, GB * (i + 1))
                pe.wait_ge(vaug_done, i + 1)
                mm(W[2][:, T:2 * T], pairs[:, :], kn[:, :, :], start=True, stop=True).then_inc(mk_ps, 1)
                if experts:
                    experts(i, 1)
                pe.wait_ge(mk_done, i + 1)
                pe.wait_ge(kv_done, GB * (i + 1))
                for b in range(GB):
                    last = mm(W[0][:, b * 2 * D:(b + 1) * 2 * D], kn[:, b, :], mkkv[:, b, :, :], start=True, stop=True)
                last.then_inc(gh_ps, 1)
                if experts:
                    experts(i, 2)
                pe.wait_ge(gh_done, i + 1)
                for b in range(GB):
                    last = mm(W[1][:, b * D:b * D + D], gh[:, b, 0, :], gh[:, b, 1, :], start=True, stop=True)
                last.then_inc(r_ps, 1)
                if experts:
                    experts(i, 3)
                pe.wait_ge(r_done, i + 1)
                pe.wait_ge(eqT_done, i + 1)
                for b in range(GB):
                    mm(W[3][:, b * D:b * D + D], eqT[:, b * S:b * S + S], r_s[:, b, :], start=True, stop=True).then_inc(attn_ps, 1)
                if experts:
                    experts(i, 4)
                pe.wait_ge(x1_done, GB * (i + 1))
                for b in range(GB):
                    last = nc.tensor.transpose(W[2][:, b * S:b * S + S], x1[:, b, :], ident[:, :])
                last.then_inc(x1T_ps, 1)
                pe.wait_ge(x1T_done, i + 1)
                mm(W[4][:, 0:T], xwq_s[:, :], x1T[:, :], start=True, stop=True).then_inc(qp_ps, 1)
                if experts:
                    experts(i, 5)
                pe.wait_ge(k_in, 16 * K_DMAS * (i + 1))
                pe.wait_ge(q_in, 16 * Q_DMAS * (i + 1))
                pe.wait_ge(zeros_in, 32 * (i + 1))
                for u in range(UNITS):
                    b, quad = u // QUADS, u % QUADS
                    if u >= 3:
                        pe.wait_ge(nm_done, UNITS * i + u - 2)
                    mm(S_BANK[u % 3][:, :], ident_b[:, :], mask4[:, :, :], start=True, stop=False, skip_group_check=True)
                    for c in range(4):
                        h = 4 * quad + c
                        last = mm(S_BANK[u % 3][:, c * S:c * S + S], q_zb[:, h % 2, h // 2, b, :], k_dn[:, h // 2, b, :],
                                  start=False, stop=(c == 3), skip_group_check=True)
                    last.then_inc(s_ps, 1)
                if experts:
                    experts(i, 6)
                pe.wait_ge(nm_done, UNITS * (i + 1))
                nc.tensor.transpose(W[2][0:NH * GB, 0:S], nm[:, :, :, :].rearrange("p r j b -> p (r j b)"), ident[:, :]).then_inc(mT_ps, 1)
                if experts:
                    experts(i, 7)
                pe.wait_ge(m_in, 16 * M_DMAS * (i + 1))
                for u in range(UNITS + 2):
                    if u < UNITS:
                        b, quad = u // QUADS, u % QUADS
                        if u >= 3:
                            pe.wait_ge(exp_done, UNITS * i + u - 2)
                        for j in range(2):
                            pair = 2 * quad + j
                            last = mm(ST_BANK[u % 3][:, j * 2 * S:(j + 1) * 2 * S], k_dn[:, pair, b, :], q_zb[:, :, pair, b, :],
                                      start=True, stop=True)
                        last.then_inc(st_ps, 1)
                    if u >= 2:
                        v = u - 2
                        b, quad = v // QUADS, v % QUADS
                        pe.wait_ge(sel_done, UNITS * i + v + 1)
                        for c in range(4):
                            last = mm(W[2 + b][K_OUT * c:K_OUT * c + K_OUT, quad * S:quad * S + S],
                                      vaug[:, b, 4 * quad + c, :], at[:, v % 3, c, :], start=True, stop=True,
                                      tile_position=(0, K_OUT * c))
                        last.then_inc(av_ps, 1)
                for b in range(GB):
                    pe.wait_ge(oT_done, GB * i + b + 1)
                    for c in range(QUADS):
                        last = nc.tensor.transpose(W[2 + b][:, c * P:c * P + P], oT[:, b, c, :], ident[:, :])
                    last.then_inc(oo_ps, 1)
                for b in range(GB):
                    pe.wait_ge(on_done, GB * i + b + 1)
                    nc.tensor.transpose(W[2 + b][:, 0:S], on[:, b, :], ident[:, :]).then_inc(onT_ps, 1)
                for b in range(GB):
                    pe.wait_ge(onT_done, GB * i + b + 1)
                    mm(W[2 + b][:, D:2 * D], onT[:, b, :], xwo_s[:, :], start=True, stop=True).then_inc(y_ps, 1)
                pe.wait_ge(x2_done, GB * (i + 1))
                for b in range(GB):
                    last = nc.tensor.transpose(W[0][:, b * S:b * S + S], x2[:, b, :], ident[:, :])
                last.then_inc(x2T_ps, 1)
                if experts is None:
                    pe.wait_ge(expert_w_in, 16 * 5)
                pe.wait_ge(x2T_done, i + 1)
                for b in range(GB):
                    last = mm(W[1][:, b * P:b * P + P], x2T[:, b * S:b * S + S], gate_s[:, :], start=True, stop=True)
                last.then_inc(lg_ps, 1)
                pe.wait_ge(gates_done, i + 1)
                for b in range(GB):
                    last = nc.tensor.transpose(W[0][:, T + b * S:T + b * S + S], gates[:, b, :], ident[:, :])
                last.then_inc(gT_ps, 1)
                pe.wait_ge(gT_done, i + 1)
                for b in range(GB):
                    last = mm(W[1][:, T + b * D:T + b * D + D], gT[:, b, :], b2_s[:, :], start=True, stop=True)
                last.then_inc(b2_ps, 1)

            attention(0, None)
            with pe.Fori(1, NG) as i:
                attention(i, experts)
            for e in range(E):
                experts(NG, e)

        @block.vector
        def _(dve):
            fills = [(ones_b, 1.0), (zero_rows, 0.0), (gate_s, 0.0), (b2_s, 0.0), (q_zb, 0.0), (vaug, 0.0), (gates, 0.0),
                     (two, LOWEST), (lg, LOWEST)]
            for tile, value in fills:
                flat = tile[tuple(slice(None) for _ in tile.shape)]
                dve.memset(flat, value).then_inc(dve_set, 1)
            dve.wait_ge(dve_set, N_FILLS)
            dve.memset(vaug[:, :, :, DH:DH + 1], 1.0).then_inc(dve_set, 1)
            dve.wait_ge(const_step, 14)
            dve.tensor_tensor(m_ones[:, :], m_tmp[:, 0:1], m_tmp[:, 1:2], ALU.add).then_inc(dve_set, 1)
            dve.wait_ge(dve_set, N_FILLS + 2)
            dve.tensor_copy(k_dn[:, :, :, :], m_ones[:, 0:1].unsqueeze(2).unsqueeze(3).broadcast_to([P, NJ, GB, S])).then_inc(consts_ready, 1)
            dve.wait_ge(bias_in, 16)
            dve.tensor_copy(bias_p[:, 0, :], bias_bc[:, :]).then_inc(bias_step, 1)
            dve.wait_ge(bias_step, 1)
            dve.tensor_tensor(bias_r[:, :], bias_bc[:, :], bias_p[:, 0, :], ALU.subtract).then_inc(bias_step, 1)
            dve.wait_ge(bias_step, 2)
            dve.tensor_copy(bias_p[:, 1, :], bias_r[:, :]).then_inc(bias_step, 1)
            dve.wait_ge(bias_step, 3)
            dve.tensor_tensor(bias_p[:, 2, :], bias_r[:, :], bias_p[:, 1, :], ALU.subtract).then_inc(bias_step, 1)
            dve.wait_ge(bias_step, 4)
            for part in range(3):
                last = dve.tensor_scalar(bias_m[:, part, :], bias_p[:, part, :], ident[:, part:part + 1], None, ALU.mult)
            last.then_inc(bias_ready, 1)

            def norm(i, src, st, mv, rstd, dst, st_done, mv_done, rstd_done, done):
                for b in range(GB):
                    last = dve.bn_stats(st[:, b, :], src[:, b, :])
                last.then_inc(st_done, 1)
                hold(dve, st_done, i + 1)
                for b in range(GB):
                    last = dve.bn_aggr(mv[:, b, :], st[:, b, :])
                last.then_inc(mv_done, 1)
                dve.wait_ge(mv_done, i + 1)
                dve.wait_ge(rstd_done, i + 1)
                for b in range(GB):
                    dve.tensor_scalar(dst[:, b, :], src[:, b, :], mv[:, b, 0:1], rstd[:, b:b + 1], ALU.subtract, ALU.mult).then_inc(done, 1)

            def hidden(i, e):
                dve.wait_ge(h_ps, E * i - E + e + 1)
                dve.wait_ge(h0_done, E * i - E + e + 1)
                dve.tensor_scalar(hs[:, e % 2, 1, :], HB[e % 2][:, T:2 * T], b1_s[:, e, 1:2], 0.0, ALU.add, ALU.max).then_inc(h1_done, 1)

            def gather(i, e):
                dve.wait_ge(ye_ps, E * i - E + e + 1)
                for b in range(GB):
                    if e:
                        dve.wait_ge(acc_done, GB * (E * i - E + e - 1) + b + 1)
                    else:
                        dve.wait_ge(acc0_done, i)
                    dve.scalar_tensor_tensor(acc[:, b, :], YB[:, b * D:b * D + D], gates[:, b, e:e + 1], acc[:, b, :],
                                             ALU.mult, ALU.add).then_inc(acc_done, 1)

            def experts(i, step):
                if step == 0:
                    hidden(i, 0)
                if step < E - 1:
                    hidden(i, step + 1)
                if step < E:
                    gather(i, step)
                if step == E - 1:
                    dve.wait_ge(acc_done, GB * E * i)
                    dve.wait_ge(gateb_in_stores, 16 * i)
                    norm(i - 1, acc, st3, mv3, rstd3, o_s, st3_done, mv3_done, rstd3_done, o_done)

            def attention(i, experts):
                for b in range(GB):
                    dve.wait_ge(qkv_ps, GB * i + b + 1)
                    wait(dve, e_done, 2 * GB * i)
                    dve.tensor_reduce(nmax1[:, b, :], W[b][:, 0:2 * D].rearrange("p (n d) -> p n d", n=2), AX, ALU.max,
                                      negate=True).then_inc(nmax_done, 1)
                dve.wait_ge(v_ps, i + 1)
                wait(dve, av_ps, UNITS * i)
                dve.tensor_copy(vaug[:, :, :, 0:DH], W[2][:, 0:T].rearrange("p (b h d) -> p b h d", b=GB, h=NH)).then_inc(vaug_done, 1)
                for b in range(GB):
                    dve.wait_ge(e_done, 2 * GB * i + 2 * b + 2)
                    dve.reciprocal(rs1[:, b, :], sum1[:, b, :]).then_inc(rs1_done, 1)
                    dve.wait_ge(rs1_done, GB * i + b + 1)
                    dve.tensor_scalar(kn[:, b, :], eqk[:, b, 1, :], rs1[:, b, 1:2], None, ALU.mult).then_inc(kn_done, 1)
                    dve.scalar_tensor_tensor(mkkv[:, b, 1, :], eqk[:, b, 1, :], rs1[:, b, 1:2], W[b][:, 2 * D:3 * D],
                                             ALU.mult, ALU.mult).then_inc(kv_done, 1)
                if experts:
                    experts(i, 0)
                    experts(i, 1)
                dve.wait_ge(gh_ps, i + 1)
                dve.tensor_copy(gh[:, :, :, :], W[0][:, :].rearrange("p (b n d) -> p b n d", b=GB, n=2)).then_inc(gh_done, 1)
                if experts:
                    experts(i, 2)
                    experts(i, 3)
                dve.wait_ge(x_in, 16 * (i + 1))
                dve.wait_ge(attn_ps, GB * (i + 1))
                for b in range(GB):
                    dve.scalar_tensor_tensor(r1[:, b, :], W[3][:, b * D:b * D + D], rs1[:, b, 0:1], x_s[:, b, :],
                                             ALU.mult, ALU.add).then_inc(r1_done, 1)
                dve.wait_ge(r1_done, GB * (i + 1))
                norm(i, r1, st1, mv1, rstd1, x1, st1_done, mv1_done, rstd1_done, x1_done)
                if experts:
                    experts(i, 4)
                dve.wait_ge(p1_done, i + 1)
                dve.tensor_tensor(rest[:, :], W[4][:, :], parts[:, 0, :, :].rearrange("p n t -> p (n t)"), ALU.subtract).then_inc(rest_done, 1)
                dve.wait_ge(p2_done, i + 1)
                dve.tensor_tensor(parts[:, 2, :, :].rearrange("p n t -> p (n t)"), rest[:, :], parts[:, 1, :, :].rearrange("p n t -> p (n t)"),
                                  ALU.subtract).then_inc(p3_done, 1)
                if experts:
                    experts(i, 5)
                for u in range(UNITS):
                    b, quad = u // QUADS, u % QUADS
                    dve.wait_ge(s_ps, UNITS * i + u + 1)
                    dve.tensor_reduce(nm[:, :, 2 * quad:2 * quad + 2, b], S_BANK[u % 3][:, :].rearrange("p (j r s) -> p r j s", j=2, r=2), AX,
                                      ALU.max, negate=True).then_inc(nm_done, 1)
                if experts:
                    experts(i, 6)
                dve.wait_ge(mT_ps, i + 1)
                wait(dve, m_in, 16 * M_DMAS * i)
                dve.tensor_copy(m_p[:, 0, :], W[2][0:NH * GB, 0:S]).then_inc(mp_step, 1)
                dve.wait_ge(mp_step, 4 * i + 1)
                dve.tensor_tensor(m_r[:, 0, :], W[2][0:NH * GB, 0:S], m_p[:, 0, :], ALU.subtract).then_inc(mp_step, 1)
                dve.wait_ge(mp_step, 4 * i + 2)
                dve.tensor_copy(m_p[:, 1, :], m_r[:, 0, :]).then_inc(mp_step, 1)
                dve.wait_ge(mp_step, 4 * i + 3)
                dve.tensor_tensor(m_p[:, 2, :], m_r[:, 0, :], m_p[:, 1, :], ALU.subtract).then_inc(mp_step, 1)
                if experts:
                    experts(i, 7)
                for b in range(GB):
                    dve.wait_ge(oo_ps, GB * i + b + 1)
                    heads = W[2 + b][:, :].rearrange("p (h k) -> p h k", k=K_OUT)
                    dve.reciprocal(rden[:, b, :], heads[:, :, DH]).then_inc(rden_done, 1)
                    dve.wait_ge(rden_done, GB * i + b + 1)
                    dve.tensor_tensor(on[:, b, :].rearrange("p (h d) -> p h d", h=NH), heads[:, :, 0:DH],
                                      rden[:, b, :].unsqueeze(2).broadcast_to([P, NH, DH]), ALU.mult).then_inc(on_done, 1)
                for b in range(GB):
                    dve.wait_ge(y_ps, GB * i + b + 1)
                    dve.tensor_tensor(r2[:, b, :], W[2 + b][:, D:2 * D], x1[:, b, :], ALU.add).then_inc(r2_done, 1)
                dve.wait_ge(r2_done, GB * (i + 1))
                norm(i, r2, st2, mv2, rstd2, x2, st2_done, mv2_done, rstd2_done, x2_done)
                if experts is None:
                    dve.wait_ge(gateb_in_stores, 16)
                dve.wait_ge(lg_ps, i + 1)
                dve.tensor_tensor(lg[:, :, 0:E], W[1][:, 0:T].rearrange("p (b e) -> p b e", b=GB)[:, :, 0:E],
                                  gateb_s[:, :].unsqueeze(1).broadcast_to([P, GB, E]), ALU.add).then_inc(lg_done, 1)
                hold(dve, lg_done, i + 1)
                for b in range(GB):
                    dve.max(top[:, b, :], lg[:, b, 0:E]).then_inc(gate_step, 1)
                dve.wait_ge(gate_step, 7 * i + 2)
                dve.tensor_copy(two[:, :, 0:2], top[:, :, 0:2]).then_inc(gate_step, 1)
                hold(dve, gate_step, 7 * i + 3)
                for b in range(GB):
                    dve.match_replace(rep[:, b, :], two[:, b, :], lg[:, b, :], LOWEST).then_inc(gate_step, 1)
                dve.tensor_tensor(lsh[:, :, :], lg[:, :, 0:E], top[:, :, 0:1].broadcast_to([P, GB, E]), ALU.subtract).then_inc(gate_step, 1)
                dve.wait_ge(gate_step, 7 * i + 6)
                dve.tensor_tensor(chosen[:, :, :], lg[:, :, 0:E], rep[:, :, 0:E], ALU.not_equal).then_inc(gate_step, 1)
                dve.wait_ge(eg_done, i + 1)
                dve.reduce_sum(gsum[:, :], eg[:, :, :], AX).then_inc(gate2, 1)
                dve.wait_ge(gate2, 3 * i + 1)
                dve.reciprocal(grec[:, :], gsum[:, :]).then_inc(gate2, 1)
                dve.wait_ge(gate_step, 7 * i + 7)
                dve.tensor_tensor(gmul[:, :, :], eg[:, :, :], chosen[:, :, :], ALU.mult).then_inc(gate2, 1)
                dve.wait_ge(gate2, 3 * i + 3)
                dve.tensor_tensor(gates[:, :, 0:E], gmul[:, :, :], grec[:, :].unsqueeze(2).broadcast_to([P, GB, E]), ALU.mult).then_inc(gates_done, 1)
                dve.wait_ge(b2_ps, i + 1)
                dve.tensor_tensor(acc[:, :, :], W[1][:, T:2 * T].rearrange("p (b d) -> p b d", b=GB), x2[:, :, :], ALU.add).then_inc(acc0_done, 1)

            attention(0, None)
            with dve.Fori(1, NG) as i:
                attention(i, experts)
            for e in range(E):
                experts(NG, e)


_ORDER = ["x", "x_t", "ctx_t", "w_qkv", "b_qkv", "xwq_t", "xwk_t", "xwv_t", "xwo_t", "gate_t", "gate_b", "w1", "b1", "w2", "b2"]


def kernel(**inputs):
    import numpy as _np
    import concourse.bacc as _bacc
    from concourse import mybir as _mybir
    from concourse.bass_utils import run_bass_kernel_spmd as _run

    a = {k: _np.asarray(v) for k, v in inputs.items()}
    nb, s, d = a["x"].shape
    e, hid = a["L0_ffn_b1"].shape
    def by_parity(w):
        return w.T.reshape(d, 8, 2, 8).transpose(0, 2, 3, 1).reshape(d, d)

    laid = {
        "x": a["x"],
        "x_t": a["x"].reshape(nb * s, d).T,
        "ctx_t": a["ctx_1024"].reshape(nb * s, d).T,
        "w_qkv": _np.stack([a["L0_attn_Wq"], a["L0_attn_Wk"], a["L0_attn_Wv"]]),
        "b_qkv": _np.concatenate([a["L0_attn_bq"], a["L0_attn_bk"], a["L0_attn_bv"]]),
        "xwq_t": by_parity(a["L0_xattn_Wq"]),
        "xwk_t": by_parity(a["L0_xattn_Wk"]),
        "xwv_t": a["L0_xattn_Wv"].T,
        "xwo_t": a["L0_xattn_Wo"].T,
        "gate_t": a["L0_ffn_gate_w"].T,
        "gate_b": a["L0_ffn_gate_b"],
        "w1": a["L0_ffn_w1"],
        "b1": a["L0_ffn_b1"].reshape(e, hid // 128, 128).transpose(2, 0, 1),
        "w2": a["L0_ffn_w2"],
        "b2": a["L0_ffn_b2"],
    }
    nc = _bacc.Bacc("TRN2", target_bir_lowering=False, num_devices=1)
    arrays, args = {}, []
    for name in _ORDER:
        v = _np.ascontiguousarray(laid[name])
        arrays[f"in_{name}"] = v
        args.append(nc.dram_tensor(f"in_{name}", v.shape, _mybir.dt.from_np(v.dtype), kind="ExternalInput").ap())
    args.append(nc.dram_tensor("out_0", a["x"].shape, _mybir.dt.float32, kind="ExternalOutput").ap())
    decoder_layer(nc, *args)
    r = _run(nc, [arrays], core_ids=[0])
    return r.results[0]["out_0"]
```

```python
import concourse.bass as bass
from concourse import mybir
from contextlib import ExitStack

F32 = mybir.dt.float32
BF16 = mybir.dt.bfloat16
F32R = mybir.dt.float32r
ALU = mybir.AluOpType
ACT = mybir.ActivationFunctionType
AX = mybir.AxisListType.X

P = 128
EPS = 1e-5
MASKED = -1e30
LOWEST = -3e38


def decoder_layer(nc, x, x_t, ctx_t, w_qkv, b_qkv, xwq_t, xwk_t, xwv_t, xwo_t, gate_t, gate_b, w1, b1, w2, b2, out):
    NB, S, D = x.shape
    E, _, HID = w1.shape
    GB = 2
    T = GB * S
    NG = NB // GB
    NH, DH = 16, 8
    NJ = NH // 2
    QUADS = NH // 4
    UNITS = GB * QUADS
    LAG = 2
    SCALE = float(DH) ** -0.5
    NHB = HID // P
    K_OUT = 32
    Q_PART = [0, 0, 0, 1, 1, 2]
    K_PART = [0, 1, 2, 0, 1, 0]
    TERMS = len(Q_PART)
    PAIR = 2 * DH
    M_ROW = TERMS * PAIR
    NMR = NJ * GB
    N_FILLS = 9
    assert D == P and S == P and NHB == 2 and M_ROW + 6 <= P

    with ExitStack() as ctx:
        def sb(name, shape, dt=F32):
            return ctx.enter_context(nc.sbuf_tensor(name, shape, dt))

        def sem(name):
            return ctx.enter_context(nc.semaphore(name))

        ident = sb("ident", [P, P])
        ident_b = sb("ident_b", [P, P], BF16)
        ones_b = sb("ones_b", [P, P], BF16)
        pairs = sb("pairs", [P, P])
        mask4 = sb("mask4", [P, 4, S], BF16)
        m_tmp = sb("m_tmp", [P, 1], BF16)
        par_tmp = sb("par_tmp", [P, P // PAIR])
        parity = sb("parity", [P, 2])
        eps_s = sb("eps_s", [P, GB])
        mhalf = sb("mhalf", [P, GB])
        wqkv_s = sb("wqkv_s", [P, 3 * D])
        bias_bc = sb("bias_bc", [P, 3 * D])
        bias_p = sb("bias_p", [P, 3, 3 * D], BF16)
        bias_r = sb("bias_r", [P, 3 * D])
        bias_t = sb("bias_t", [P, 2, 3 * D], BF16)
        bias_m = sb("bias_m", [P, 3 * D], BF16)
        xwq_s = sb("xwq_s", [P, D])
        xwk_s = sb("xwk_s", [P, D])
        xwv_s = sb("xwv_s", [P, D])
        xwo_s = sb("xwo_s", [P, D])
        gate_s = sb("gate_s", [P, P])
        gateb_s = sb("gateb_s", [P, E])
        w1_s = sb("w1_s", [P, E, HID])
        w1_hi = sb("w1_hi", [P, E, HID], F32R)
        w1_lo = sb("w1_lo", [P, E, HID], F32R)
        b1_s = sb("b1_s", [P, E, NHB])
        w2_s = sb("w2_s", [P, E, NHB, D])
        b2_s = sb("b2_s", [P, D])
        x_s = sb("x_s", [P, GB, D])
        xT_s = sb("xT_s", [P, T])
        nmax1 = sb("nmax1", [P, GB, 2])
        eqk = sb("eqk", [P, GB, 2, D])
        sum1 = sb("sum1", [P, GB, 2])
        rs1 = sb("rs1", [P, GB, 2])
        kn = sb("kn", [P, GB, D])
        mkkv = sb("mkkv", [P, GB, 2, D])
        eqT = sb("eqT", [P, T])
        gh = sb("gh", [P, GB, 2, D])
        r_s = sb("r_s", [P, GB, D])
        r1 = sb("r1", [P, GB, D])
        x1 = sb("x1", [P, 2, GB, D])
        x1T = sb("x1T", [P, T])
        cT_s = sb("cT_s", [P, T])
        vaug = sb("vaug", [P, GB, NH, K_OUT])
        parts = sb("parts", [P, 3, 2, T], BF16)
        rest = sb("rest", [P, 2 * T])
        q_dn = sb("q_dn", [P, NJ, GB, S], BF16)
        q_zb = sb("q_zb", [P, 2, NJ, GB, S], BF16)
        k_dn = sb("k_dn", [P, NJ, GB, S], BF16)
        nm = sb("nm", [P, 2, NJ, GB])
        nm_r = sb("nm_r", [P, 2, NJ, GB])
        nm_p = sb("nm_p", [P, 2, 3, NMR], BF16)
        mT = sb("mT", [2 * 3 * NMR, S], BF16)
        at = sb("at", [P, 3, 4, S])
        oT = sb("oT", [P, GB, QUADS, S])
        rden = sb("rden", [P, GB, NH])
        on = sb("on", [P, GB, D])
        onT = sb("onT", [P, GB, S])
        r2 = sb("r2", [P, GB, D])
        x2 = sb("x2", [P, GB, D])
        x2T = sb("x2T", [P, T])
        x2_hi = sb("x2_hi", [P, T], F32R)
        x2_lo = sb("x2_lo", [P, T], F32R)
        lg = sb("lg", [P, GB, 2 * E])
        top = sb("top", [P, GB, 8])
        two = sb("two", [P, GB, 8])
        rep = sb("rep", [P, GB, 2 * E])
        chosen = sb("chosen", [P, GB, E])
        lsh = sb("lsh", [P, GB, E])
        eg = sb("eg", [P, GB, E])
        gsum = sb("gsum", [P, GB])
        grec = sb("grec", [P, GB])
        gmul = sb("gmul", [P, GB, E])
        gates = sb("gates", [P, GB, P])
        gT = sb("gT", [P, GB, S])
        hs = sb("hs", [P, 2, NHB, T])
        acc = sb("acc", [P, GB, D])
        o_s = sb("o_s", [P, GB, D])
        stats = [sb(f"stats{n}", [P, GB, 6]) for n in range(3)]
        mv = [sb(f"mv{n}", [P, GB, 2]) for n in range(3)]
        veps = [sb(f"veps{n}", [P, GB]) for n in range(3)]
        rstd = [sb(f"rstd{n}", [P, GB]) for n in range(3)]

        W = [ctx.enter_context(nc.psum_tensor(f"W{n}", [P, 512], F32)) for n in range(5)]
        HB = [ctx.enter_context(nc.psum_tensor(f"HB{n}", [P, 512], F32)) for n in range(2)]
        YB = ctx.enter_context(nc.psum_tensor("YB", [P, 512], F32))

        const_step, dve_set, consts_ready = sem("const_step"), sem("dve_set"), sem("consts_ready")
        bias_in, bias_step, bias_ready = sem("bias_in"), sem("bias_step"), sem("bias_ready")
        attn_w_in, xattn_w_in, expert_w_in = sem("attn_w_in"), sem("xattn_w_in"), sem("expert_w_in")
        w1_hi_done, w1_lo_done = sem("w1_hi_done"), sem("w1_lo_done")
        x_in, xT_in, cT_in, q_in, k_in, m_in = (sem(n) for n in ("x_in", "xT_in", "cT_in", "q_in", "k_in", "m_in"))
        gateb_in_stores = sem("gateb_in_stores")
        qkv_ps, mk_ps, eqT_ps, gh_ps, r_ps, attn_ps = (sem(n) for n in ("qkv_ps", "mk_ps", "eqT_ps", "gh_ps", "r_ps", "attn_ps"))
        x1T_ps, kp_ps, qp_ps, v_ps = (sem(n) for n in ("x1T_ps", "kp_ps", "qp_ps", "v_ps"))
        s_ps, mT_ps, st_ps, av_ps, oo_ps, onT_ps, y_ps = (sem(n) for n in ("s_ps", "mT_ps", "st_ps", "av_ps", "oo_ps", "onT_ps", "y_ps"))
        x2T_ps, lg_ps, gT_ps, b2_ps, h_ps, ye_ps = (sem(n) for n in ("x2T_ps", "lg_ps", "gT_ps", "b2_ps", "h_ps", "ye_ps"))
        e_done, mk_done, eqT_done, r_done, x1T_done = (sem(n) for n in ("e_done", "mk_done", "eqT_done", "r_done", "x1T_done"))
        p1_done, p2_done, exp_done, oT_done, onT_done, mT_done = (sem(n) for n in ("p1_done", "p2_done", "exp_done", "oT_done", "onT_done", "mT_done"))
        x2T_done, x2_hi_done, eg_done, gT_done, h0_done = (sem(n) for n in ("x2T_done", "x2_hi_done", "eg_done", "gT_done", "h0_done"))
        nmax_done, rs1_done, kn_done, kv_done, gh_done, r1_done, x1_done = (
            sem(n) for n in ("nmax_done", "rs1_done", "kn_done", "kv_done", "gh_done", "r1_done", "x1_done"))
        vaug_done, rest_done, p3_done, q_zb_done, nm_done, nm_step = (
            sem(n) for n in ("vaug_done", "rest_done", "p3_done", "q_zb_done", "nm_done", "nm_step"))
        rden_done, on_done, r2_done, x2_done, x2_lo_done = (sem(n) for n in ("rden_done", "on_done", "r2_done", "x2_done", "x2_lo_done"))
        lg_done, top_step, sum_step, gates_done, acc0_done = (sem(n) for n in ("lg_done", "top_step", "sum_step", "gates_done", "acc0_done"))
        h1_done, acc_done, o_done = sem("h1_done"), sem("acc_done"), sem("o_done")
        stats_done = [sem(f"stats{n}_done") for n in range(3)]
        mv_done = [sem(f"mv{n}_done") for n in range(3)]
        sel_done = sem("sel_done")
        veps_done = [sem(f"veps{n}_done") for n in range(3)]
        rstd_done = [sem(f"rstd{n}_done") for n in range(3)]

        def wait(eng, s, value):
            if not (isinstance(value, int) and value <= 0):
                eng.wait_ge(s, value)

        def hold(eng, s, value):
            at_least = value if isinstance(value, int) else eng.snap(eng.to_reg(value))
            eng.wait_ge(consts_ready, 1)
            eng.wait_ge(s, at_least)

        def waits(eng, *pairs):
            known = [(s, v if isinstance(v, int) else eng.snap(eng.to_reg(v))) for s, v in pairs]
            for s, v in known:
                wait(eng, s, v)

        def turn(t, par, do):
            def run(step, back, *more):
                if not isinstance(t, int) or 0 <= t - back < NG:
                    do(step, t - back, (par + back) % 2, *more)

            run("gate_logits", 2)
            run("expert_start", 2)
            run("project", 0)
            run("spread_q", 1)
            run("score_maxima", 1, 0, UNITS // 2)
            run("gate_bias", 2)
            run("expert", 2, 0)
            run("score_maxima", 1, UNITS // 2, UNITS)
            run("split_maxima", 1)
            run("landmarks", 0)
            run("expert", 2, 1)
            run("send_maxima", 1)
            run("load_next", -1)
            run("key_products", 0)
            run("expert", 2, 2)
            run("combine_products", 0)
            run("expert", 2, 3)
            run("self_output", 0)
            run("attend", 1, 0, UNITS // 2 + 1)
            run("expert", 2, 4)
            run("project_q_k", 0)
            run("attend", 1, UNITS // 2 + 1, UNITS + LAG)
            run("expert", 2, 5)
            run("split_q_k", 0)
            run("stack_q_k", 0)
            run("normalise", 1)
            run("project_v", 0)
            run("expert", 2, 6)
            run("cross_output", 1)
            run("expert", 2, 7)
            run("expert_end", 2)
            run("transpose_x2", 1)

        LOOP = (3, NG - 1)

        def pipeline(eng, do):
            for t in range(LOOP[0]):
                turn(t, t % 2, do)
            with eng.Fori(LOOP[0], LOOP[1] - 1, 2) as t:
                turn(t, LOOP[0] % 2, do)
                turn(t + 1, (LOOP[0] + 1) % 2, do)
            for t in range(LOOP[1], NG + 2):
                turn(t, t % 2, do)

        assert (LOOP[1] - LOOP[0]) % 2 == 0
        block = ctx.enter_context(nc.Block())

        @block.sync
        def _(sp):
            def load_tokens(g):
                wait(sp, qkv_ps, g * GB)
                sp.dma_start(xT_s[:, :], x_t[:, bass.ds(g * T, T)]).then_inc(xT_in, 16)
                wait(sp, r1_done, g * GB)
                sp.dma_start(x_s[:, :, :], x[bass.ds(g * GB, GB), :, :].rearrange("b s d -> s b d")).then_inc(x_in, 16)

            def load_context(g):
                waits(sp, (v_ps, g), (kp_ps, g))
                sp.dma_start(cT_s[:, :], ctx_t[:, bass.ds(g * T, T)]).then_inc(cT_in, 16)

            def do(step, g, par, *more):
                if step == "send_maxima":
                    sp.wait_ge(mT_done, g + 1)
                    for n in range(2):
                        sp.dma_start(q_zb[M_ROW + 3 * n:M_ROW + 3 * n + 3, n, :, :, :].rearrange("p j b s -> p (j b s)"),
                                     mT[3 * NMR * n:3 * NMR * (n + 1), :]).then_inc(m_in, 16)
                elif step == "load_next" and not (isinstance(g, int) and g == 0):
                    load_tokens(g)
                elif step == "stack_q_k":
                    waits(sp, (q_zb_done, 2 * g), (st_ps, UNITS * g), (p1_done, g + 1))
                    for part, done in ((0, None), (1, p2_done), (2, p3_done)):
                        if done:
                            sp.wait_ge(done, g + 1)
                        for n in range(TERMS):
                            rows = slice(PAIR * n, PAIR * n + PAIR)
                            if Q_PART[n] == part:
                                sp.dma_start(q_dn[rows, :, :, :].rearrange("d j b s -> d j (b s)"), parts[:, part, 0, :]).then_inc(q_in, 16)
                            if K_PART[n] == part:
                                sp.dma_start(k_dn[rows, :, :, :].rearrange("d j b s -> d j (b s)"), parts[:, part, 1, :]).then_inc(k_in, 16)
                elif step == "project_v" and not (isinstance(g, int) and g == NG - 1):
                    load_context(g + 1)

            sp.dma_start(wqkv_s[:, :].rearrange("p (w n) -> p w n", w=3), w_qkv.rearrange("w p n -> p w n")).then_inc(attn_w_in, 16)
            load_tokens(0)
            load_context(0)
            sp.dma_start(xwk_s[:, :], xwk_t).then_inc(xattn_w_in, 16)
            sp.dma_start(xwv_s[:, :], xwv_t).then_inc(xattn_w_in, 16)
            sp.dma_start(xwq_s[:, :], xwq_t).then_inc(xattn_w_in, 16)
            sp.dma_start(xwo_s[:, :], xwo_t).then_inc(xattn_w_in, 16)
            sp.wait_ge(dve_set, 3)
            sp.dma_start(gate_s[:, 0:E], gate_t).then_inc(expert_w_in, 16)
            sp.dma_start(b2_s[0:E, :], b2).then_inc(expert_w_in, 16)
            sp.dma_start(b1_s[:, :, :], b1).then_inc(expert_w_in, 16)
            sp.dma_start(w1_s[:, :, :], w1.rearrange("e d h -> d e h")).then_inc(expert_w_in, 16)
            sp.dma_start(w2_s[:, :, :, :], w2.rearrange("e (n p) o -> p e n o", p=P)).then_inc(expert_w_in, 16)
            sp.wait_ge(consts_ready, 1)
            pipeline(sp, do)

        @block.gpsimd
        def _(pool):
            pool.dma_start(bias_bc[:, :], b_qkv.rearrange("(o n) -> o n", o=1).broadcast_to([P, 3 * D])).then_inc(bias_in, 16)
            pool.dma_start(gateb_s[:, :], gate_b.rearrange("(o n) -> o n", o=1).broadcast_to([P, E])).then_inc(gateb_in_stores, 16)
            for tile, value in ((ident, 0.0), (ident_b, 0.0), (pairs, 0.25), (mask4, 0.0), (m_tmp, 1.0), (par_tmp, 1.0),
                                (eps_s, EPS), (mhalf, -0.5)):
                pool.memset(tile[tuple(slice(None) for _ in tile.shape)], value).then_inc(const_step, 1)
            pool.wait_ge(const_step, 8)
            for m in (ident, ident_b):
                pool.affine_select(out=m[:, :], in_=m[:, :], compare_op=ALU.not_equal, fill=1.0, base=0,
                                   pattern=[[-1, P]], channel_multiplier=1).then_inc(const_step, 1)
            pv = pairs[:, :].rearrange("p (j w) -> p j w", w=2)
            pool.affine_select(out=pv, in_=pv, compare_op=ALU.is_ge, fill=0.0, base=0,
                               pattern=[[-2, P // 2], [0, 2]], channel_multiplier=1).then_inc(const_step, 1)
            pool.affine_select(out=mask4[:, :, :], in_=mask4[:, :, :], compare_op=ALU.is_ge, fill=MASKED, base=0,
                               pattern=[[0, 4], [-1, S]], channel_multiplier=1).then_inc(const_step, 1)
            pool.affine_select(out=m_tmp[:, :], in_=m_tmp[:, :], compare_op=ALU.is_ge, fill=0.0,
                               base=-M_ROW, pattern=[[0, 1]], channel_multiplier=1).then_inc(const_step, 1)
            pool.affine_select(out=par_tmp[:, :], in_=par_tmp[:, :], compare_op=ALU.is_ge, fill=0.0,
                               base=0, pattern=[[-PAIR, P // PAIR]], channel_multiplier=1).then_inc(const_step, 1)
            pool.wait_ge(const_step, 14)
            pool.affine_select(out=pv, in_=pv, compare_op=ALU.is_ge, fill=0.0, base=1,
                               pattern=[[2, P // 2], [0, 2]], channel_multiplier=-1).then_inc(const_step, 1)
            pool.affine_select(out=m_tmp[:, :], in_=m_tmp[:, :], compare_op=ALU.is_ge, fill=0.0,
                               base=M_ROW + 5, pattern=[[0, 1]], channel_multiplier=-1).then_inc(const_step, 1)
            pool.affine_select(out=par_tmp[:, :], in_=par_tmp[:, :], compare_op=ALU.is_ge, fill=0.0,
                               base=DH - 1, pattern=[[PAIR, P // PAIR]], channel_multiplier=-1).then_inc(const_step, 1)

            def inverse_deviation(g, n):
                pool.wait_ge(mv_done[n], g + 1)
                pool.tensor_tensor(veps[n][:, :], mv[n][:, :, 1], eps_s[:, :], ALU.add).then_inc(veps_done[n], 1)
                pool.wait_ge(veps_done[n], g + 1)
                pool.tensor_tensor(rstd[n][:, :], veps[n][:, :], mhalf[:, :], ALU.pow).then_inc(rstd_done[n], 1)

            def do(step, g, par, *more):
                if step == "self_output":
                    inverse_deviation(g, 0)
                elif step == "attend":
                    for u in range(max(more[0] - 1, 0), min(more[1] - 1, UNITS)):
                        hold(pool, exp_done, UNITS * g + u + 1)
                        pool.affine_select(out=at[:, u % 3, :, :], in_=at[:, u % 3, :, :], compare_op=ALU.is_ge, fill=0.0,
                                           base=0, pattern=[[0, 4], [1, S]], channel_multiplier=-1).then_inc(sel_done, 1)
                elif step == "cross_output":
                    inverse_deviation(g, 1)
                elif step == "expert_end":
                    inverse_deviation(g, 2)
                    hold(pool, o_done, GB * (g + 1))
                    pool.dma_start(out[bass.ds(g * GB, GB), :, :].rearrange("b s d -> s b d"), o_s[:, :, :]).then_inc(gateb_in_stores, 16)

            pipeline(pool, do)
            pool.wait_ge(gateb_in_stores, 16 * (NG + 1))

        @block.scalar
        def _(act):
            def hidden(g, e):
                act.wait_ge(h_ps, E * g + e + 1)
                act.activation(hs[:, e % 2, 0, :], HB[e % 2][:, 0:T], ACT.Relu, bias=b1_s[:, e, 0:1]).then_inc(h0_done, 1)

            def do(step, g, par, *more):
                if step == "expert_start":
                    hidden(g, 0)
                elif step == "expert" and more[0] < E - 1:
                    hidden(g, more[0] + 1)
                elif step == "project":
                    for b in range(GB):
                        act.wait_ge(nmax_done, GB * g + b + 1)
                        if b == 0:
                            wait(act, eqT_ps, g)
                            wait(act, kv_done, GB * g)
                            wait(act, x1_done, GB * g)
                        for n in range(2):
                            act.activation(eqk[:, b, n, :], W[3 + b][:, n * D:n * D + D], ACT.Exp, bias=nmax1[:, b, n:n + 1],
                                           accum_out=sum1[:, b, n:n + 1]).then_inc(e_done, 1)
                elif step == "gate_bias":
                    act.wait_ge(gT_ps, g + 1)
                    act.activation(gT[:, :, :], W[2][:, 0:T].rearrange("p (b s) -> p b s", b=GB), ACT.Copy).then_inc(gT_done, 1)
                elif step == "gate_logits":
                    act.wait_ge(top_step, 7 * g + 6)
                    act.activation(eg[:, :, :], lsh[:, :, :], ACT.Exp).then_inc(eg_done, 1)
                elif step == "landmarks":
                    act.wait_ge(eqT_ps, g + 1)
                    act.activation(eqT[:, :], W[0][:, 0:T], ACT.Copy).then_inc(eqT_done, 1)
                    act.wait_ge(mk_ps, g + 1)
                    act.activation(mkkv[:, :, 0, :], W[1][:, 0:T].rearrange("p (b d) -> p b d", b=GB), ACT.Copy).then_inc(mk_done, 1)
                elif step == "send_maxima":
                    act.wait_ge(mT_ps, g + 1)
                    act.activation(mT[:, :], W[2][0:2 * 3 * NMR, 0:S // 2].bitcast(BF16), ACT.Copy).then_inc(mT_done, 1)
                elif step == "combine_products":
                    act.wait_ge(r_ps, g + 1)
                    act.activation(r_s[:, :, :], W[1][:, 0:T].rearrange("p (b d) -> p b d", b=GB), ACT.Copy).then_inc(r_done, 1)
                elif step == "project_q_k":
                    act.wait_ge(x1T_ps, g + 1)
                    act.activation(x1T[:, :], W[4][:, 0:T], ACT.Copy).then_inc(x1T_done, 1)
                elif step == "split_q_k":
                    act.wait_ge(kp_ps, g + 1)
                    act.wait_ge(qp_ps, g + 1)
                    wait(act, q_in, 16 * TERMS * g)
                    wait(act, k_in, 16 * TERMS * g)
                    act.activation(parts[:, 0, :, :], W[4][:, :].rearrange("p (n t) -> p n t", n=2), ACT.Copy).then_inc(p1_done, 1)
                    act.wait_ge(rest_done, g + 1)
                    act.activation(parts[:, 1, :, :], rest[:, :].rearrange("p (n t) -> p n t", n=2), ACT.Copy).then_inc(p2_done, 1)
                elif step == "attend":
                    for u in range(more[0], min(more[1], UNITS)):
                        act.wait_ge(st_ps, UNITS * g + u + 1)
                        wait(act, av_ps, UNITS * g + u - 2)
                        act.activation(at[:, u % 3, :, :], W[u % 2][:, :].rearrange("p (h s) -> p h s", h=4),
                                       ACT.Exp, scale=SCALE).then_inc(exp_done, 1)
                elif step == "normalise":
                    for b in range(GB):
                        act.wait_ge(av_ps, UNITS * g + QUADS * (b + 1))
                        act.activation(oT[:, b, :, :], W[2 + b][:, :].rearrange("p (c s) -> p c s", c=QUADS), ACT.Copy).then_inc(oT_done, 1)
                elif step == "cross_output":
                    for b in range(GB):
                        act.wait_ge(onT_ps, GB * g + b + 1)
                        act.activation(onT[:, b, :], W[2 + b][:, 0:S], ACT.Copy).then_inc(onT_done, 1)
                elif step == "transpose_x2":
                    act.wait_ge(x2T_ps, g + 1)
                    act.activation(x2_hi[:, :], W[1][:, 0:T], ACT.Copy).then_inc(x2_hi_done, 1)
                    act.activation(x2T[:, :], W[1][:, 0:T], ACT.Copy).then_inc(x2T_done, 1)

            act.wait_ge(consts_ready, 1)
            act.wait_ge(expert_w_in, 16 * 5)
            act.activation(w1_hi[:, :, :], w1_s[:, :, :], ACT.Copy).then_inc(w1_hi_done, 1)
            pipeline(act, do)

        @block.tensor
        def _(pe):
            mm = nc.tensor.matmul

            def hidden(g, e):
                if e >= 2:
                    pe.wait_ge(h0_done, E * g + e - 1)
                    pe.wait_ge(h1_done, E * g + e - 1)
                for n in range(NHB):
                    block_n = slice(n * P, n * P + P)
                    for w, v in ((w1_lo, x2_hi), (w1_hi, x2_lo), (w1_hi, x2_hi)):
                        last = mm(HB[e % 2][:, n * T:n * T + T], w[:, e, block_n], v[:, :], start=(w is w1_lo), stop=(w is w1_hi and v is x2_hi))
                last.then_inc(h_ps, 1)

            def expert_out(g, e):
                pe.wait_ge(h0_done, E * g + e + 1)
                pe.wait_ge(h1_done, E * g + e + 1)
                if e == 0:
                    pe.wait_ge(acc0_done, g + 1)
                else:
                    pe.wait_ge(acc_done, GB * (E * g + e))
                for b in range(GB):
                    for n in range(NHB):
                        last = mm(YB[:, b * D:b * D + D], hs[:, e % 2, n, b * S:b * S + S], w2_s[:, e, n, :],
                                  start=(n == 0), stop=(n == NHB - 1))
                last.then_inc(ye_ps, 1)

            def do(step, g, par, *more):
                first = isinstance(g, int) and g == 0
                if step == "gate_logits":
                    pe.wait_ge(x2T_done, g + 1)
                    for b in range(GB):
                        last = mm(W[2][:, b * P:b * P + P], x2T[:, b * S:b * S + S], gate_s[:, :], start=True, stop=True)
                    last.then_inc(lg_ps, 1)
                elif step == "expert_start":
                    pe.wait_ge(x2_hi_done, g + 1)
                    pe.wait_ge(x2_lo_done, g + 1)
                    hidden(g, 0)
                elif step == "expert":
                    if more[0] < E - 1:
                        hidden(g, more[0] + 1)
                    expert_out(g, more[0])
                elif step == "project":
                    pe.wait_ge(xT_in, 16 * (g + 1))
                    if first:
                        pe.wait_ge(attn_w_in, 16)
                        pe.wait_ge(bias_ready, 1)
                        pe.wait_ge(consts_ready, 1)
                    wait(pe, rest_done, g)
                    wait(pe, r2_done, GB * (g - 1))
                    for b in range(GB):
                        mm(W[3 + b][:, 0:3 * D], xT_s[:, b * S:b * S + S], wqkv_s[:, :], start=True, stop=False)
                        mm(W[3 + b][:, 0:3 * D], ones_b[:, :], bias_m[:, :], start=False, stop=True).then_inc(qkv_ps, 1)
                elif step == "score_maxima":
                    if more[0] == 0:
                        pe.wait_ge(k_in, 16 * TERMS * (g + 1))
                        pe.wait_ge(q_zb_done, 2 * (g + 1))
                        pe.wait_ge(vaug_done, g + 1)
                        wait(pe, x2T_done, g)
                        wait(pe, x2_lo_done, g)
                    for u in range(*more):
                        b, quad = u // QUADS, u % QUADS
                        if u >= 2:
                            pe.wait_ge(nm_done, UNITS * g + u - 1)
                        mm(W[u % 2][:, :], ident_b[:, :], mask4[:, :, :], start=True, stop=False, skip_group_check=True)
                        for c in range(4):
                            h = 4 * quad + c
                            last = mm(W[u % 2][:, c * S:c * S + S], q_zb[:, h % 2, h // 2, b, :], k_dn[:, h // 2, b, :],
                                      start=False, stop=(c == 3), skip_group_check=True)
                        last.then_inc(s_ps, 1)
                elif step == "gate_bias":
                    pe.wait_ge(gates_done, g + 1)
                    for b in range(GB):
                        last = nc.tensor.transpose(W[2][:, b * S:b * S + S], gates[:, b, :], ident[:, :])
                    last.then_inc(gT_ps, 1)
                    pe.wait_ge(gT_done, g + 1)
                    for b in range(GB):
                        last = mm(W[2][:, T + b * D:T + b * D + D], gT[:, b, :], b2_s[:, :], start=True, stop=True)
                    last.then_inc(b2_ps, 1)
                elif step == "landmarks":
                    pe.wait_ge(e_done, 2 * GB * (g + 1))
                    wait(pe, nm_done, UNITS * g)
                    for b in range(GB):
                        last = nc.tensor.transpose(W[0][:, b * S:b * S + S], eqk[:, b, 0, :], ident[:, :])
                    last.then_inc(eqT_ps, 1)
                    pe.wait_ge(kn_done, GB * (g + 1))
                    mm(W[1][:, 0:T], pairs[:, :], kn[:, :, :], start=True, stop=True).then_inc(mk_ps, 1)
                elif step == "send_maxima":
                    pe.wait_ge(nm_step, 4 * (g + 1))
                    wait(pe, acc0_done, g)
                    nc.tensor.transpose(W[2][0:2 * 3 * NMR, 0:S // 2].bitcast(BF16), nm_p[:, :, :, :].rearrange("p n k r -> p (n k r)"),
                                        ident_b[:, :]).then_inc(mT_ps, 1)
                elif step == "key_products":
                    pe.wait_ge(mk_done, g + 1)
                    pe.wait_ge(eqT_done, g + 1)
                    pe.wait_ge(kv_done, GB * (g + 1))
                    for b in range(GB):
                        last = mm(W[0][:, b * 2 * D:(b + 1) * 2 * D], kn[:, b, :], mkkv[:, b, :, :], start=True, stop=True)
                    last.then_inc(gh_ps, 1)
                elif step == "combine_products":
                    pe.wait_ge(gh_done, g + 1)
                    for b in range(GB):
                        last = mm(W[1][:, b * D:b * D + D], gh[:, b, 0, :], gh[:, b, 1, :], start=True, stop=True)
                    last.then_inc(r_ps, 1)
                elif step == "self_output":
                    pe.wait_ge(r_done, g + 1)
                    wait(pe, mT_done, g)
                    for b in range(GB):
                        last = mm(W[2][:, b * D:b * D + D], eqT[:, b * S:b * S + S], r_s[:, b, :], start=True, stop=True)
                    last.then_inc(attn_ps, 1)
                elif step == "project_q_k":
                    pe.wait_ge(x1_done, GB * (g + 1))
                    for b in range(GB):
                        last = nc.tensor.transpose(W[4][:, b * S:b * S + S], x1[:, par, b, :], ident[:, :])
                    last.then_inc(x1T_ps, 1)
                    pe.wait_ge(cT_in, 16 * (g + 1))
                    if first:
                        pe.wait_ge(xattn_w_in, 64)
                    pe.wait_ge(x1T_done, g + 1)
                    mm(W[4][:, T:2 * T], xwk_s[:, :], cT_s[:, :], start=True, stop=True).then_inc(kp_ps, 1)
                    mm(W[4][:, 0:T], xwq_s[:, :], x1T[:, :], start=True, stop=True).then_inc(qp_ps, 1)
                elif step == "attend":
                    if more[0] == 0:
                        pe.wait_ge(m_in, 16 * 2 * (g + 1))
                        if not (isinstance(g, int) and g + 1 >= NG):
                            pe.wait_ge(gh_done, g + 2)
                            pe.wait_ge(r_done, g + 2)
                            pe.wait_ge(r1_done, GB * (g + 2))
                    for u in range(*more):
                        if u < UNITS:
                            b, quad = u // QUADS, u % QUADS
                            if u >= 2:
                                pe.wait_ge(exp_done, UNITS * g + u - 1)
                            for j in range(2):
                                pair = 2 * quad + j
                                last = mm(W[u % 2][:, j * 2 * S:(j + 1) * 2 * S], k_dn[:, pair, b, :], q_zb[:, :, pair, b, :],
                                          start=True, stop=True)
                            last.then_inc(st_ps, 1)
                        if u >= LAG:
                            v = u - LAG
                            b, quad = v // QUADS, v % QUADS
                            pe.wait_ge(sel_done, UNITS * g + v + 1)
                            for c in range(4):
                                last = mm(W[2 + b][K_OUT * c:K_OUT * c + K_OUT, quad * S:quad * S + S],
                                          vaug[:, b, 4 * quad + c, :], at[:, v % 3, c, :], start=True, stop=True,
                                          tile_position=(0, K_OUT * c))
                            last.then_inc(av_ps, 1)
                elif step == "project_v":
                    wait(pe, exp_done, UNITS * g)
                    for b in range(GB):
                        last = mm(W[0][:, b * D:b * D + D], cT_s[:, b * S:b * S + S], xwv_s[:, :], start=True, stop=True)
                    last.then_inc(v_ps, 1)
                elif step == "normalise":
                    for b in range(GB):
                        pe.wait_ge(oT_done, GB * g + b + 1)
                        for c in range(QUADS):
                            last = nc.tensor.transpose(W[2 + b][:, c * P:c * P + P], oT[:, b, c, :], ident[:, :])
                        last.then_inc(oo_ps, 1)
                elif step == "cross_output":
                    for b in range(GB):
                        pe.wait_ge(on_done, GB * g + b + 1)
                        nc.tensor.transpose(W[2 + b][:, 0:S], on[:, b, :], ident[:, :]).then_inc(onT_ps, 1)
                    for b in range(GB):
                        pe.wait_ge(onT_done, GB * g + b + 1)
                        mm(W[2 + b][:, D:2 * D], onT[:, b, :], xwo_s[:, :], start=True, stop=True).then_inc(y_ps, 1)
                elif step == "transpose_x2":
                    pe.wait_ge(x2_done, GB * (g + 1))
                    pe.wait_ge(exp_done, UNITS * (g + 1))
                    if first:
                        pe.wait_ge(expert_w_in, 16 * 5)
                        pe.wait_ge(w1_lo_done, 1)
                    for b in range(GB):
                        last = nc.tensor.transpose(W[1][:, b * S:b * S + S], x2[:, b, :], ident[:, :])
                    last.then_inc(x2T_ps, 1)

            pipeline(pe, do)

        @block.vector
        def _(dve):
            fills = [(ones_b, 1.0), (gate_s, 0.0), (b2_s, 0.0), (q_dn, 0.0), (vaug, 0.0), (gates, 0.0),
                     (two, LOWEST), (lg, LOWEST), (nm_p, 0.0)]
            for tile, value in fills:
                dve.memset(tile[tuple(slice(None) for _ in tile.shape)], value).then_inc(dve_set, 1)
            dve.wait_ge(dve_set, N_FILLS)
            dve.memset(vaug[:, :, :, DH:DH + 1], 1.0).then_inc(dve_set, 1)
            dve.wait_ge(const_step, 17)
            dve.tensor_copy(k_dn[:, :, :, :], m_tmp[:, 0:1].unsqueeze(2).unsqueeze(3).broadcast_to([P, NJ, GB, S])).then_inc(dve_set, 1)
            dve.reduce_sum(parity[:, 0:1], par_tmp[:, :], AX).then_inc(dve_set, 1)
            dve.wait_ge(dve_set, N_FILLS + 3)
            dve.tensor_scalar(parity[:, 1:2], parity[:, 0:1], -1.0, 1.0, ALU.mult, ALU.add).then_inc(consts_ready, 1)
            dve.wait_ge(bias_in, 16)
            dve.tensor_copy(bias_p[:, 0, :], bias_bc[:, :]).then_inc(bias_step, 1)
            dve.wait_ge(bias_step, 1)
            dve.tensor_tensor(bias_r[:, :], bias_bc[:, :], bias_p[:, 0, :], ALU.subtract).then_inc(bias_step, 1)
            dve.wait_ge(bias_step, 2)
            dve.tensor_copy(bias_p[:, 1, :], bias_r[:, :]).then_inc(bias_step, 1)
            dve.wait_ge(bias_step, 3)
            dve.tensor_tensor(bias_p[:, 2, :], bias_r[:, :], bias_p[:, 1, :], ALU.subtract).then_inc(bias_step, 1)
            dve.tensor_scalar(bias_t[:, 0, :], bias_p[:, 0, :], ident[:, 0:1], None, ALU.mult).then_inc(bias_step, 1)
            dve.wait_ge(bias_step, 5)
            dve.scalar_tensor_tensor(bias_t[:, 1, :], bias_p[:, 1, :], ident[:, 1:2], bias_t[:, 0, :], ALU.mult, ALU.add).then_inc(bias_step, 1)
            dve.wait_ge(bias_step, 6)
            dve.scalar_tensor_tensor(bias_m[:, :], bias_p[:, 2, :], ident[:, 2:3], bias_t[:, 1, :], ALU.mult, ALU.add).then_inc(bias_ready, 1)

            def norm(g, n, src, dst, done):
                for b in range(GB):
                    last = dve.bn_stats(stats[n][:, b, :], src[:, b, :])
                last.then_inc(stats_done[n], 1)
                hold(dve, stats_done[n], g + 1)
                for b in range(GB):
                    last = dve.bn_aggr(mv[n][:, b, :], stats[n][:, b, :])
                last.then_inc(mv_done[n], 1)
                dve.wait_ge(rstd_done[n], g + 1)
                for b in range(GB):
                    dve.tensor_scalar(dst[:, b, :], src[:, b, :], mv[n][:, b, 0:1], rstd[n][:, b:b + 1], ALU.subtract, ALU.mult).then_inc(done, 1)

            def hidden(g, e):
                dve.wait_ge(h0_done, E * g + e + 1)
                dve.tensor_scalar(hs[:, e % 2, 1, :], HB[e % 2][:, T:2 * T], b1_s[:, e, 1:2], 0.0, ALU.add, ALU.max).then_inc(h1_done, 1)

            def gather(g, e):
                dve.wait_ge(ye_ps, E * g + e + 1)
                for b in range(GB):
                    if e:
                        dve.wait_ge(acc_done, GB * (E * g + e - 1) + b + 1)
                    else:
                        dve.wait_ge(acc0_done, g + 1)
                    dve.scalar_tensor_tensor(acc[:, b, :], YB[:, b * D:b * D + D], gates[:, b, e:e + 1], acc[:, b, :],
                                             ALU.mult, ALU.add).then_inc(acc_done, 1)

            def do(step, g, par, *more):
                if step == "gate_logits":
                    dve.wait_ge(lg_ps, g + 1)
                    dve.tensor_tensor(lg[:, :, 0:E], W[2][:, 0:T].rearrange("p (b e) -> p b e", b=GB)[:, :, 0:E],
                                      gateb_s[:, :].unsqueeze(1).broadcast_to([P, GB, E]), ALU.add).then_inc(lg_done, 1)
                    hold(dve, lg_done, g + 1)
                    for b in range(GB):
                        dve.max(top[:, b, :], lg[:, b, 0:E]).then_inc(top_step, 1)
                    dve.wait_ge(top_step, 7 * g + 2)
                    dve.tensor_copy(two[:, :, 0:2], top[:, :, 0:2]).then_inc(top_step, 1)
                    dve.tensor_tensor(lsh[:, :, :], lg[:, :, 0:E], top[:, :, 0:1].broadcast_to([P, GB, E]), ALU.subtract).then_inc(top_step, 1)
                    hold(dve, top_step, 7 * g + 4)
                    for b in range(GB):
                        dve.match_replace(rep[:, b, :], two[:, b, :], lg[:, b, :], LOWEST).then_inc(top_step, 1)
                    dve.wait_ge(top_step, 7 * g + 6)
                    dve.tensor_tensor(chosen[:, :, :], lg[:, :, 0:E], rep[:, :, 0:E], ALU.not_equal).then_inc(top_step, 1)
                    dve.wait_ge(eg_done, g + 1)
                    dve.reduce_sum(gsum[:, :], eg[:, :, :], AX).then_inc(sum_step, 1)
                    dve.wait_ge(sum_step, 3 * g + 1)
                    dve.reciprocal(grec[:, :], gsum[:, :]).then_inc(sum_step, 1)
                    dve.wait_ge(top_step, 7 * g + 7)
                    dve.tensor_tensor(gmul[:, :, :], eg[:, :, :], chosen[:, :, :], ALU.mult).then_inc(sum_step, 1)
                    dve.wait_ge(sum_step, 3 * g + 3)
                    dve.tensor_tensor(gates[:, :, 0:E], gmul[:, :, :], grec[:, :].unsqueeze(2).broadcast_to([P, GB, E]), ALU.mult).then_inc(gates_done, 1)
                elif step == "expert_start":
                    hidden(g, 0)
                elif step == "gate_bias":
                    dve.wait_ge(b2_ps, g + 1)
                    dve.tensor_tensor(acc[:, :, :], W[2][:, T:2 * T].rearrange("p (b d) -> p b d", b=GB), x2[:, :, :], ALU.add).then_inc(acc0_done, 1)
                elif step == "expert":
                    if more[0] < E - 1:
                        hidden(g, more[0] + 1)
                    gather(g, more[0])
                elif step == "expert_end":
                    dve.wait_ge(acc_done, GB * E * (g + 1))
                    dve.wait_ge(gateb_in_stores, 16 * (g + 1))
                    norm(g, 2, acc, o_s, o_done)
                elif step == "project":
                    for b in range(GB):
                        dve.wait_ge(qkv_ps, GB * g + b + 1)
                        wait(dve, e_done, 2 * GB * g)
                        dve.tensor_reduce(nmax1[:, b, :], W[3 + b][:, 0:2 * D].rearrange("p (n d) -> p n d", n=2), AX, ALU.max,
                                          negate=True).then_inc(nmax_done, 1)
                elif step == "spread_q":
                    dve.wait_ge(q_in, 16 * TERMS * (g + 1))
                    wait(dve, st_ps, UNITS * g)
                    for n in range(2):
                        dve.tensor_scalar(q_zb[:, n, :, :, :], q_dn[:, :, :, :], parity[:, n:n + 1], None, ALU.mult).then_inc(q_zb_done, 1)
                elif step == "score_maxima":
                    for u in range(*more):
                        b, quad = u // QUADS, u % QUADS
                        dve.wait_ge(s_ps, UNITS * g + u + 1)
                        dve.tensor_reduce(nm[:, :, 2 * quad:2 * quad + 2, b], W[u % 2][:, :].rearrange("p (j r s) -> p r j s", j=2, r=2), AX,
                                          ALU.max, negate=True).then_inc(nm_done, 1)
                elif step == "split_maxima":
                    dve.wait_ge(nm_done, UNITS * (g + 1))
                    wait(dve, mT_ps, g)
                    src = nm[:, :, :, :].rearrange("p n j b -> p n (j b)")
                    res = nm_r[:, :, :, :].rearrange("p n j b -> p n (j b)")
                    dve.tensor_copy(nm_p[:, :, 0, :], src).then_inc(nm_step, 1)
                    dve.wait_ge(nm_step, 4 * g + 1)
                    dve.tensor_tensor(res, src, nm_p[:, :, 0, :], ALU.subtract).then_inc(nm_step, 1)
                    dve.wait_ge(nm_step, 4 * g + 2)
                    dve.tensor_copy(nm_p[:, :, 1, :], res).then_inc(nm_step, 1)
                    dve.wait_ge(nm_step, 4 * g + 3)
                    dve.tensor_tensor(nm_p[:, :, 2, :], res, nm_p[:, :, 1, :], ALU.subtract).then_inc(nm_step, 1)
                elif step == "landmarks":
                    for b in range(GB):
                        dve.wait_ge(e_done, 2 * GB * g + 2 * b + 2)
                        dve.reciprocal(rs1[:, b, :], sum1[:, b, :]).then_inc(rs1_done, 1)
                        dve.wait_ge(rs1_done, GB * g + b + 1)
                        dve.tensor_scalar(kn[:, b, :], eqk[:, b, 1, :], rs1[:, b, 1:2], None, ALU.mult).then_inc(kn_done, 1)
                    for b in range(GB):
                        dve.scalar_tensor_tensor(mkkv[:, b, 1, :], eqk[:, b, 1, :], rs1[:, b, 1:2], W[3 + b][:, 2 * D:3 * D],
                                                 ALU.mult, ALU.mult).then_inc(kv_done, 1)
                elif step == "key_products":
                    dve.wait_ge(gh_ps, g + 1)
                    dve.tensor_copy(gh[:, :, :, :], W[0][:, :].rearrange("p (b n d) -> p b n d", b=GB, n=2)).then_inc(gh_done, 1)
                elif step == "self_output":
                    dve.wait_ge(x_in, 16 * (g + 1))
                    dve.wait_ge(attn_ps, g + 1)
                    for b in range(GB):
                        dve.scalar_tensor_tensor(r1[:, b, :], W[2][:, b * D:b * D + D], rs1[:, b, 0:1], x_s[:, b, :],
                                                 ALU.mult, ALU.add).then_inc(r1_done, 1)
                    dve.wait_ge(r1_done, GB * (g + 1))
                    norm(g, 0, r1, x1[:, par, :, :], x1_done)
                elif step == "split_q_k":
                    dve.wait_ge(p1_done, g + 1)
                    dve.tensor_tensor(rest[:, :], W[4][:, :], parts[:, 0, :, :].rearrange("p n t -> p (n t)"), ALU.subtract).then_inc(rest_done, 1)
                    dve.wait_ge(p2_done, g + 1)
                    dve.tensor_tensor(parts[:, 2, :, :].rearrange("p n t -> p (n t)"), rest[:, :], parts[:, 1, :, :].rearrange("p n t -> p (n t)"),
                                      ALU.subtract).then_inc(p3_done, 1)
                elif step == "project_v":
                    dve.wait_ge(v_ps, g + 1)
                    dve.tensor_copy(vaug[:, :, :, 0:DH], W[0][:, 0:T].rearrange("p (b h d) -> p b h d", b=GB, h=NH)).then_inc(vaug_done, 1)
                elif step == "normalise":
                    for b in range(GB):
                        dve.wait_ge(oo_ps, GB * g + b + 1)
                        heads = W[2 + b][:, :].rearrange("p (h k) -> p h k", k=K_OUT)
                        dve.reciprocal(rden[:, b, :], heads[:, :, DH]).then_inc(rden_done, 1)
                        dve.wait_ge(rden_done, GB * g + b + 1)
                        dve.tensor_tensor(on[:, b, :].rearrange("p (h d) -> p h d", h=NH), heads[:, :, 0:DH],
                                          rden[:, b, :].unsqueeze(2).broadcast_to([P, NH, DH]), ALU.mult).then_inc(on_done, 1)
                elif step == "cross_output":
                    for b in range(GB):
                        dve.wait_ge(y_ps, GB * g + b + 1)
                        dve.tensor_tensor(r2[:, b, :], W[2 + b][:, D:2 * D], x1[:, par, b, :], ALU.add).then_inc(r2_done, 1)
                    dve.wait_ge(r2_done, GB * (g + 1))
                    norm(g, 1, r2, x2, x2_done)
                    if isinstance(g, int) and g == 0:
                        dve.wait_ge(w1_hi_done, 1)
                        dve.tensor_tensor(w1_lo[:, :, :], w1_s[:, :, :], w1_hi[:, :, :].bitcast(F32), ALU.subtract).then_inc(w1_lo_done, 1)
                elif step == "transpose_x2":
                    dve.wait_ge(x2T_done, g + 1)
                    dve.tensor_tensor(x2_lo[:, :], W[1][:, 0:T], x2_hi[:, :].bitcast(F32), ALU.subtract).then_inc(x2_lo_done, 1)

            dve.wait_ge(gateb_in_stores, 16)
            pipeline(dve, do)


_ORDER = ["x", "x_t", "ctx_t", "w_qkv", "b_qkv", "xwq_t", "xwk_t", "xwv_t", "xwo_t", "gate_t", "gate_b", "w1", "b1", "w2", "b2"]


def kernel(**inputs):
    import numpy as _np
    import concourse.bacc as _bacc
    from concourse import mybir as _mybir
    from concourse.bass_utils import run_bass_kernel_spmd as _run

    a = {k: _np.asarray(v) for k, v in inputs.items()}
    nb, s, d = a["x"].shape
    e, hid = a["L0_ffn_b1"].shape
    def by_parity(w):
        return w.T.reshape(d, 8, 2, 8).transpose(0, 2, 3, 1).reshape(d, d)

    laid = {
        "x": a["x"],
        "x_t": a["x"].reshape(nb * s, d).T,
        "ctx_t": a["ctx_1024"].reshape(nb * s, d).T,
        "w_qkv": _np.stack([a["L0_attn_Wq"], a["L0_attn_Wk"], a["L0_attn_Wv"]]),
        "b_qkv": _np.concatenate([a["L0_attn_bq"], a["L0_attn_bk"], a["L0_attn_bv"]]),
        "xwq_t": by_parity(a["L0_xattn_Wq"]),
        "xwk_t": by_parity(a["L0_xattn_Wk"]),
        "xwv_t": a["L0_xattn_Wv"].T,
        "xwo_t": a["L0_xattn_Wo"].T,
        "gate_t": a["L0_ffn_gate_w"].T,
        "gate_b": a["L0_ffn_gate_b"],
        "w1": a["L0_ffn_w1"],
        "b1": a["L0_ffn_b1"].reshape(e, hid // 128, 128).transpose(2, 0, 1),
        "w2": a["L0_ffn_w2"],
        "b2": a["L0_ffn_b2"],
    }
    nc = _bacc.Bacc("TRN2", target_bir_lowering=False, num_devices=1)
    arrays, args = {}, []
    for name in _ORDER:
        v = _np.ascontiguousarray(laid[name])
        arrays[f"in_{name}"] = v
        args.append(nc.dram_tensor(f"in_{name}", v.shape, _mybir.dt.from_np(v.dtype), kind="ExternalInput").ap())
    args.append(nc.dram_tensor("out_0", a["x"].shape, _mybir.dt.float32, kind="ExternalOutput").ap())
    decoder_layer(nc, *args)
    r = _run(nc, [arrays], core_ids=[0])
    return r.results[0]["out_0"]
```

```python
import concourse.bass as bass
from concourse import mybir
from contextlib import ExitStack

F32 = mybir.dt.float32
BF16 = mybir.dt.bfloat16
F32R = mybir.dt.float32r
ALU = mybir.AluOpType
ACT = mybir.ActivationFunctionType
AX = mybir.AxisListType.X

P = 128
EPS = 1e-5
MASKED = -1e30
LOWEST = -3e38


def decoder_layer(nc, x, x_t, ctx_t, w_qkv, b_qkv, xwq_t, xwk_t, xwv_t, xwo_t, gate_t, gate_b, w1, b1, w2, b2, out):
    NB, S, D = x.shape
    E, _, HID = w1.shape
    GB = 2
    T = GB * S
    NG = NB // GB
    NH, DH = 16, 8
    NJ = NH // 2
    QUADS = NH // 4
    UNITS = GB * QUADS
    LAG = 2
    SCALE = float(DH) ** -0.5
    NHB = HID // P
    K_OUT = 32
    Q_PART = [0, 0, 0, 1, 1, 2]
    K_PART = [0, 1, 2, 0, 1, 0]
    TERMS = len(Q_PART)
    PAIR = 2 * DH
    M_ROW = TERMS * PAIR
    NMR = NJ * GB
    N_FILLS = 6
    HALVED = 3
    OUTS = E + GB - 1
    OUT_BY = [e + (GB - 1) * (e > HALVED) for e in range(E)]
    assert D == P and S == P and NHB == 2 and M_ROW + 6 <= P

    with ExitStack() as ctx:
        def sb(name, shape, dt=F32):
            return ctx.enter_context(nc.sbuf_tensor(name, shape, dt))

        def sem(name):
            return ctx.enter_context(nc.semaphore(name))

        ident = sb("ident", [P, P])
        ident_b = sb("ident_b", [P, P], BF16)
        pairs = sb("pairs", [P, P])
        mask4 = sb("mask4", [P, 4, S], BF16)
        par_tmp = sb("par_tmp", [P, P // PAIR])
        parity = sb("parity", [P, 2])
        eps_s = sb("eps_s", [P, GB])
        mhalf = sb("mhalf", [P, GB])
        wqkv_s = sb("wqkv_s", [P, 3 * D])
        bias_bc = sb("bias_bc", [P, 3 * D])
        xwq_s = sb("xwq_s", [P, D])
        xwk_s = sb("xwk_s", [P, D])
        xwv_s = sb("xwv_s", [P, D])
        xwo_s = sb("xwo_s", [P, D])
        gate_s = sb("gate_s", [P, P])
        gateb_s = sb("gateb_s", [P, E])
        w1_s = sb("w1_s", [P, E, HID])
        w1_hi = sb("w1_hi", [P, E, HID], F32R)
        w1_lo = sb("w1_lo", [P, E, HID], F32R)
        b1_s = sb("b1_s", [P, E, NHB])
        w2_s = sb("w2_s", [P, E, NHB, D])
        b2_s = sb("b2_s", [P, D])
        x_s = sb("x_s", [P, GB, D])
        xT_s = sb("xT_s", [P, T])
        qkv = sb("qkv", [P, GB, 3 * D])
        nmax1 = sb("nmax1", [P, GB, 2])
        eqk = sb("eqk", [P, GB, 2, D])
        sum1 = sb("sum1", [P, GB, 2])
        rs1 = sb("rs1", [P, GB, 2])
        kn = sb("kn", [P, GB, D])
        mkkv = sb("mkkv", [P, GB, 2, D])
        eqT = sb("eqT", [P, T])
        gh = sb("gh", [P, GB, 2, D])
        r_s = sb("r_s", [P, GB, D])
        r1 = sb("r1", [P, GB, D])
        x1 = sb("x1", [P, 2, GB, D])
        x1T = sb("x1T", [P, T])
        cT_s = sb("cT_s", [P, T])
        vaug = sb("vaug", [P, GB, NH, K_OUT])
        parts = sb("parts", [P, 2, 3, T], BF16)
        rest = sb("rest", [P, 2, T])
        q_dn = sb("q_dn", [P, NJ, GB, S], BF16)
        q_zb = sb("q_zb", [P, 2, NJ, GB, S], BF16)
        k_dn = sb("k_dn", [P, 2, NJ, GB, S], BF16)
        nm = sb("nm", [P, 2, NJ, GB])
        nm_r = sb("nm_r", [P, 2, NJ, GB])
        nm_p = sb("nm_p", [P, 2, 3, NMR], BF16)
        mT = sb("mT", [2 * 3 * NMR, S], BF16)
        at = sb("at", [P, 3, 4, S])
        oT = sb("oT", [P, GB, QUADS, S])
        rden = sb("rden", [P, GB, NH])
        on = sb("on", [P, GB, D])
        onT = sb("onT", [P, GB, S])
        r2 = sb("r2", [P, GB, D])
        x2 = sb("x2", [P, GB, D])
        x2T = sb("x2T", [P, T])
        x2_hi = sb("x2_hi", [P, T], F32R)
        x2_lo = sb("x2_lo", [P, T], F32R)
        lg = sb("lg", [P, GB, 2 * E])
        top = sb("top", [P, GB, 8])
        two = sb("two", [P, GB, 8])
        rep = sb("rep", [P, GB, 2 * E])
        chosen = sb("chosen", [P, GB, E])
        lsh = sb("lsh", [P, GB, E])
        eg = sb("eg", [P, GB, E])
        gsum = sb("gsum", [P, GB])
        grec = sb("grec", [P, GB])
        gmul = sb("gmul", [P, GB, E])
        gates = sb("gates", [P, GB, P])
        gT = sb("gT", [P, GB, S])
        hs = sb("hs", [P, 2, NHB, T])
        acc = sb("acc", [P, 2, GB, D])
        o_s = sb("o_s", [P, GB, D])
        stats = [sb(f"stats{n}", [P, GB, 6]) for n in range(3)]
        mv = [sb(f"mv{n}", [P, GB, 2]) for n in range(3)]
        veps = [sb(f"veps{n}", [P, GB]) for n in range(3)]
        rstd = [sb(f"rstd{n}", [P, GB]) for n in range(3)]

        W = [ctx.enter_context(nc.psum_tensor(f"W{n}", [P, 512], F32)) for n in range(5)]
        HB = [ctx.enter_context(nc.psum_tensor(f"HB{n}", [P, 512], F32)) for n in range(2)]
        YB = ctx.enter_context(nc.psum_tensor("YB", [P, 512], F32))

        const_step, dve_set, consts_ready = sem("const_step"), sem("dve_set"), sem("consts_ready")
        k_filled, q_v_filled = sem("k_filled"), sem("q_v_filled")
        bias_in = sem("bias_in")
        attn_w_in, xattn_w_in, expert_w_in = sem("attn_w_in"), sem("xattn_w_in"), sem("expert_w_in")
        w1_hi_done, w1_lo_done = sem("w1_hi_done"), sem("w1_lo_done")
        x_in, xT_in, cT_in, q_in, k_in, m_in = (sem(n) for n in ("x_in", "xT_in", "cT_in", "q_in", "k_in", "m_in"))
        gateb_in_stores = sem("gateb_in_stores")
        qkv_ps, mk_ps, eqT_ps, gh_ps, r_ps, attn_ps = (sem(n) for n in ("qkv_ps", "mk_ps", "eqT_ps", "gh_ps", "r_ps", "attn_ps"))
        x1T_ps, kq_ps, v_ps = (sem(n) for n in ("x1T_ps", "kq_ps", "v_ps"))
        s_ps, mT_ps, st_ps, av_ps, oo_ps, onT_ps, y_ps = (sem(n) for n in ("s_ps", "mT_ps", "st_ps", "av_ps", "oo_ps", "onT_ps", "y_ps"))
        x2T_ps, lg_ps, gT_ps, b2_ps, h_ps, ye_ps = (sem(n) for n in ("x2T_ps", "lg_ps", "gT_ps", "b2_ps", "h_ps", "ye_ps"))
        e_done, mk_done, eqT_done, r_done, x1T_done = (sem(n) for n in ("e_done", "mk_done", "eqT_done", "r_done", "x1T_done"))
        p1_done, p2_done, exp_done, oT_done, onT_done, mT_done = (sem(n) for n in ("p1_done", "p2_done", "exp_done", "oT_done", "onT_done", "mT_done"))
        x2T_done, x2_hi_done, eg_done, gT_done, h_done = (sem(n) for n in ("x2T_done", "x2_hi_done", "eg_done", "gT_done", "h_done"))
        qkv_done, nmax_done, rs1_done, kn_done, kv_done, gh_done, r1_done, x1_done = (
            sem(n) for n in ("qkv_done", "nmax_done", "rs1_done", "kn_done", "kv_done", "gh_done", "r1_done", "x1_done"))
        vaug_done, rest_done, p3_done, q_zb_done, nm_done, nm_step = (
            sem(n) for n in ("vaug_done", "rest_done", "p3_done", "q_zb_done", "nm_done", "nm_step"))
        rden_done, on_done, r2_done, x2_done, x2_lo_done = (sem(n) for n in ("rden_done", "on_done", "r2_done", "x2_done", "x2_lo_done"))
        lg_done, top_step, sum_step, gates_done, bias_done = (sem(n) for n in ("lg_done", "top_step", "sum_step", "gates_done", "bias_done"))
        acc_done, o_done = sem("acc_done"), sem("o_done")
        stats_done = [sem(f"stats{n}_done") for n in range(3)]
        mv_done = [sem(f"mv{n}_done") for n in range(3)]
        sel_done = sem("sel_done")
        veps_done = [sem(f"veps{n}_done") for n in range(3)]
        rstd_done = [sem(f"rstd{n}_done") for n in range(3)]

        def wait(eng, s, value):
            if not (isinstance(value, int) and value <= 0):
                eng.wait_ge(s, value)

        def hold(eng, s, value):
            at_least = value if isinstance(value, int) else eng.snap(eng.to_reg(value))
            eng.wait_ge(consts_ready, 1)
            eng.wait_ge(s, at_least)

        def waits(eng, *pairs):
            known = [(s, v if isinstance(v, int) else eng.snap(eng.to_reg(v))) for s, v in pairs]
            for s, v in known:
                wait(eng, s, v)

        def turn(t, par, steps, do):
            for step, back, *more in steps:
                if not isinstance(t, int) or 0 <= t - back < NG:
                    do(step, t - back, (par + back) % 2, *more)

        LOOP = (3, NG - 1)

        def pipeline(eng, steps, do):
            for t in range(LOOP[0]):
                turn(t, t % 2, steps, do)
            with eng.Fori(LOOP[0], LOOP[1] - 1, 2) as t:
                turn(t, LOOP[0] % 2, steps, do)
                turn(t + 1, (LOOP[0] + 1) % 2, steps, do)
            for t in range(LOOP[1], NG + 3):
                turn(t, t % 2, steps, do)

        assert (LOOP[1] - LOOP[0]) % 2 == 0
        block = ctx.enter_context(nc.Block())

        @block.sync
        def _(sp):
            def load_tokens_t(g):
                wait(sp, qkv_ps, g * GB)
                sp.dma_start(xT_s[:, :], x_t[:, bass.ds(g * T, T)]).then_inc(xT_in, 16)

            def load_tokens(g):
                wait(sp, r1_done, g * GB)
                sp.dma_start(x_s[:, :, :], x[bass.ds(g * GB, GB), :, :].rearrange("b s d -> s b d")).then_inc(x_in, 16)

            def load_context(g):
                waits(sp, (v_ps, g), (kq_ps, 2 * g))
                sp.dma_start(cT_s[:, :], ctx_t[:, bass.ds(g * T, T)]).then_inc(cT_in, 16)

            def do(step, g, par, *more):
                if step == "send_maxima":
                    sp.wait_ge(mT_done, g + 1)
                    for n in range(2):
                        sp.dma_start(q_zb[M_ROW + 3 * n:M_ROW + 3 * n + 3, n, :, :, :].rearrange("p j b s -> p (j b s)"),
                                     mT[3 * NMR * n:3 * NMR * (n + 1), :]).then_inc(m_in, 16)
                elif step == "load_next":
                    load_tokens_t(g)
                elif step == "load_next_x":
                    load_tokens(g)
                elif step == "other_parts":
                    q = more[0]
                    if isinstance(g, int) and g == 0:
                        sp.wait_ge(k_filled, 1)
                        sp.wait_ge(q_v_filled, 3)
                    if q:
                        waits(sp, (q_zb_done, 2 * g), (p1_done, 2 * g + 2))
                    else:
                        waits(sp, (st_ps, UNITS * (g - 1)), (p1_done, 2 * g + 1))
                    for part, done in ((0, None), (1, p2_done), (2, p3_done)):
                        if done:
                            sp.wait_ge(done, 2 * g + 1 + q)
                        for n in range(TERMS):
                            rows = slice(PAIR * n, PAIR * n + PAIR)
                            if (Q_PART if q else K_PART)[n] == part:
                                dst = q_dn[rows, :, :, :] if q else k_dn[rows, par, :, :, :]
                                sp.dma_start(dst.rearrange("d j b s -> d j (b s)"), parts[:, q, part, :]).then_inc(q_in if q else k_in, 16)
                elif step == "project_v" and not (isinstance(g, int) and g == NG - 1):
                    load_context(g + 1)

            sp.dma_start(wqkv_s[:, :].rearrange("p (w n) -> p w n", w=3), w_qkv.rearrange("w p n -> p w n")).then_inc(attn_w_in, 16)
            load_tokens_t(0)
            load_tokens(0)
            load_context(0)
            sp.dma_start(xwk_s[:, :], xwk_t).then_inc(xattn_w_in, 16)
            sp.dma_start(xwv_s[:, :], xwv_t).then_inc(xattn_w_in, 16)
            sp.dma_start(xwq_s[:, :], xwq_t).then_inc(xattn_w_in, 16)
            sp.dma_start(xwo_s[:, :], xwo_t).then_inc(xattn_w_in, 16)
            sp.wait_ge(dve_set, 2)
            sp.dma_start(gate_s[:, 0:E], gate_t).then_inc(expert_w_in, 16)
            sp.dma_start(b2_s[0:E, :], b2).then_inc(expert_w_in, 16)
            sp.dma_start(b1_s[:, :, :], b1).then_inc(expert_w_in, 16)
            sp.dma_start(w1_s[:, :, :], w1.rearrange("e d h -> d e h")).then_inc(expert_w_in, 16)
            sp.dma_start(w2_s[:, :, :, :], w2.rearrange("e (n p) o -> p e n o", p=P)).then_inc(expert_w_in, 16)
            sp.wait_ge(consts_ready, 1)
            steps = [
                ("load_next", -1), ("project_v", 1), ("send_maxima", 1), ("other_parts", 0, 0), ("load_next_x", -1),
                ("other_parts", 0, 1),
            ]
            pipeline(sp, steps, do)

        @block.gpsimd
        def _(pool):
            pool.dma_start(bias_bc[:, :], b_qkv.rearrange("(o n) -> o n", o=1).broadcast_to([P, 3 * D])).then_inc(bias_in, 16)
            pool.dma_start(gateb_s[:, :], gate_b.rearrange("(o n) -> o n", o=1).broadcast_to([P, E])).then_inc(gateb_in_stores, 16)
            for tile, value in ((ident, 0.0), (ident_b, 0.0), (pairs, 0.25), (mask4, 0.0), (par_tmp, 1.0),
                                (eps_s, EPS), (mhalf, -0.5)):
                pool.memset(tile[tuple(slice(None) for _ in tile.shape)], value).then_inc(const_step, 1)
            pool.wait_ge(const_step, 7)
            for m in (ident, ident_b):
                pool.affine_select(out=m[:, :], in_=m[:, :], compare_op=ALU.not_equal, fill=1.0, base=0,
                                   pattern=[[-1, P]], channel_multiplier=1).then_inc(const_step, 1)
            pv = pairs[:, :].rearrange("p (j w) -> p j w", w=2)
            pool.affine_select(out=pv, in_=pv, compare_op=ALU.is_ge, fill=0.0, base=0,
                               pattern=[[-2, P // 2], [0, 2]], channel_multiplier=1).then_inc(const_step, 1)
            pool.affine_select(out=par_tmp[:, :], in_=par_tmp[:, :], compare_op=ALU.is_ge, fill=0.0,
                               base=0, pattern=[[-PAIR, P // PAIR]], channel_multiplier=1).then_inc(const_step, 1)
            pool.wait_ge(const_step, 11)
            pool.affine_select(out=pv, in_=pv, compare_op=ALU.is_ge, fill=0.0, base=1,
                               pattern=[[2, P // 2], [0, 2]], channel_multiplier=-1).then_inc(const_step, 1)
            pool.affine_select(out=par_tmp[:, :], in_=par_tmp[:, :], compare_op=ALU.is_ge, fill=0.0,
                               base=DH - 1, pattern=[[PAIR, P // PAIR]], channel_multiplier=-1).then_inc(const_step, 1)
            pool.affine_select(out=mask4[:, :, :], in_=mask4[:, :, :], compare_op=ALU.is_ge, fill=MASKED, base=0,
                               pattern=[[0, 4], [-1, S]], channel_multiplier=1).then_inc(const_step, 1)
            pool.memset(vaug[:, :, :, :], 0.0).then_inc(q_v_filled, 1)
            pool.wait_ge(q_v_filled, 1)
            pool.memset(vaug[:, :, :, DH:DH + 1], 1.0).then_inc(q_v_filled, 1)
            pool.wait_ge(q_v_filled, 2)
            pool.memset(q_dn[M_ROW:P, :, :, :], 0.0).then_inc(q_v_filled, 1)
            pool.memset(k_dn[M_ROW:P, :, :, :, :], 1.0).then_inc(k_filled, 1)
            pool.wait_ge(q_v_filled, 3)
            pool.wait_ge(k_filled, 1)

            def inverse_deviation(g, n):
                pool.wait_ge(mv_done[n], g + 1)
                pool.tensor_tensor(veps[n][:, :], mv[n][:, :, 1], eps_s[:, :], ALU.add).then_inc(veps_done[n], 1)
                pool.wait_ge(veps_done[n], g + 1)
                pool.tensor_tensor(rstd[n][:, :], veps[n][:, :], mhalf[:, :], ALU.pow).then_inc(rstd_done[n], 1)

            def do(step, g, par, *more):
                if step == "deviation_x1":
                    inverse_deviation(g, 0)
                elif step == "attend":
                    for u in [more[0] - 1] if 1 <= more[0] <= UNITS else []:
                        hold(pool, exp_done, UNITS * g + u + 1)
                        pool.affine_select(out=at[:, u % 3, :, :], in_=at[:, u % 3, :, :], compare_op=ALU.is_ge, fill=0.0,
                                           base=0, pattern=[[0, 4], [1, S]], channel_multiplier=-1).then_inc(sel_done, 1)
                elif step == "moments_x2":
                    inverse_deviation(g, 1)
                elif step == "moments_out":
                    inverse_deviation(g, 2)
                elif step == "keep_v" and isinstance(g, int) and g == 0:
                    pool.wait_ge(w1_hi_done, 1)
                    pool.tensor_tensor(w1_lo[:, :, :], w1_s[:, :, :], w1_hi[:, :, :].bitcast(F32), ALU.subtract).then_inc(w1_lo_done, 1)
                elif step == "split_x2":
                    pool.wait_ge(x2T_done, g + 1)
                    pool.wait_ge(x2_hi_done, g + 1)
                    pool.tensor_tensor(x2_lo[:, :], x2T[:, :], x2_hi[:, :].bitcast(F32), ALU.subtract).then_inc(x2_lo_done, 1)
                elif step == "store":
                    hold(pool, o_done, GB * (g + 1))
                    pool.dma_start(out[bass.ds(g * GB, GB), :, :].rearrange("b s d -> s b d"), o_s[:, :, :]).then_inc(gateb_in_stores, 16)

            steps = [
                ("moments_x2", 2), ("split_x2", 2), ("moments_out", 3), ("attend", 1, 1), ("deviation_x1", 0),
                ("attend", 1, 2), ("attend", 1, 3), ("attend", 1, 4), ("attend", 1, 5), ("store", 3), ("keep_v", 0),
                ("attend", 1, 6), ("attend", 1, 7), ("attend", 1, 8),
            ]
            pipeline(pool, steps, do)
            pool.wait_ge(gateb_in_stores, 16 * (NG + 1))

        @block.scalar
        def _(act):
            def do(step, g, par, *more):
                if step == "hidden":
                    e = more[0]
                    act.wait_ge(h_ps, E * g + e + 1)
                    for n in range(NHB):
                        act.activation(hs[:, e % 2, n, :], HB[e % 2][:, n * T:n * T + T], ACT.Relu, bias=b1_s[:, e, n:n + 1]).then_inc(h_done, 1)
                elif step == "feature_maxima":
                    for b in range(GB):
                        act.wait_ge(nmax_done, GB * g + b + 1)
                        if b == 0:
                            wait(act, eqT_ps, g)
                            wait(act, kv_done, GB * g)
                            wait(act, x1_done, GB * g)
                        for n in range(2):
                            act.activation(eqk[:, b, n, :], qkv[:, b, n * D:n * D + D], ACT.Exp, bias=nmax1[:, b, n:n + 1],
                                           accum_out=sum1[:, b, n:n + 1]).then_inc(e_done, 1)
                elif step == "transpose_gates":
                    act.wait_ge(gT_ps, g + 1)
                    act.activation(gT[:, :, :], W[3][:, 0:T].rearrange("p (b s) -> p b s", b=GB), ACT.Copy).then_inc(gT_done, 1)
                elif step == "weigh":
                    act.wait_ge(top_step, 7 * g + 6)
                    act.activation(eg[:, :, :], lsh[:, :, :], ACT.Exp).then_inc(eg_done, 1)
                elif step == "keep_k":
                    for b in range(GB):
                        act.wait_ge(rs1_done, GB * g + b + 1)
                        act.activation(kn[:, b, :], eqk[:, b, 1, :], ACT.Copy, scale=rs1[:, b, 1:2]).then_inc(kn_done, 1)
                elif step == "landmarks":
                    act.wait_ge(eqT_ps, g + 1)
                    act.activation(eqT[:, :], W[0][:, 0:T], ACT.Copy).then_inc(eqT_done, 1)
                    act.wait_ge(mk_ps, g + 1)
                    act.activation(mkkv[:, :, 0, :], W[1][:, 0:T].rearrange("p (b d) -> p b d", b=GB), ACT.Copy).then_inc(mk_done, 1)
                elif step == "send_maxima":
                    act.wait_ge(mT_ps, g + 1)
                    act.activation(mT[:, :], W[3][0:2 * 3 * NMR, 0:S // 2].bitcast(BF16), ACT.Copy).then_inc(mT_done, 1)
                elif step == "key_products":
                    act.wait_ge(gh_ps, g + 1)
                    act.activation(gh[:, :, :, :], W[0][:, :].rearrange("p (b n d) -> p b n d", b=GB, n=2), ACT.Copy).then_inc(gh_done, 1)
                elif step == "combine_products":
                    act.wait_ge(r_ps, g + 1)
                    act.activation(r_s[:, :, :], W[1][:, 0:T].rearrange("p (b d) -> p b d", b=GB), ACT.Copy).then_inc(r_done, 1)
                elif step == "transpose_x1":
                    act.wait_ge(x1T_ps, g + 1)
                    act.activation(x1T[:, :], W[4][:, 0:T], ACT.Copy).then_inc(x1T_done, 1)
                elif step == "first_part":
                    q = more[0]
                    act.wait_ge(kq_ps, 2 * g + 1 + q)
                    wait(act, q_in if q else k_in, 16 * TERMS * g)
                    act.activation(parts[:, q, 0, :], W[4][:, T * q:T * q + T], ACT.Copy).then_inc(p1_done, 1)
                elif step == "other_parts":
                    q = more[0]
                    act.wait_ge(rest_done, 2 * g + 1 + q)
                    act.activation(parts[:, q, 1, :], rest[:, q, :], ACT.Copy).then_inc(p2_done, 1)
                elif step == "attend":
                    for u in more if more[0] < UNITS else []:
                        act.wait_ge(st_ps, UNITS * g + u + 1)
                        wait(act, av_ps, UNITS * g + u - 2)
                        act.activation(at[:, u % 3, :, :], W[u % 2][:, :].rearrange("p (h s) -> p h s", h=4),
                                       ACT.Exp, scale=SCALE).then_inc(exp_done, 1)
                elif step == "collect":
                    for b in more:
                        act.wait_ge(av_ps, UNITS * g + QUADS * (b + 1))
                        act.activation(oT[:, b, :, :], W[2 + b][:, :].rearrange("p (c s) -> p c s", c=QUADS), ACT.Copy).then_inc(oT_done, 1)
                elif step == "transpose_on":
                    for b in more:
                        act.wait_ge(onT_ps, GB * g + b + 1)
                        act.activation(onT[:, b, :], W[2 + b][:, 0:S], ACT.Copy).then_inc(onT_done, 1)
                elif step == "keep_v":
                    if isinstance(g, int) and g == 0:
                        act.wait_ge(q_v_filled, 2)
                    wait(act, av_ps, UNITS * g)
                    act.wait_ge(v_ps, g + 1)
                    act.activation(vaug[:, :, :, 0:DH], W[0][:, 0:T].rearrange("p (b h d) -> p b h d", b=GB, h=NH), ACT.Copy).then_inc(vaug_done, 1)
                    if isinstance(g, int) and g == 0:
                        act.wait_ge(expert_w_in, 16 * 5)
                        act.activation(w1_hi[:, :, :], w1_s[:, :, :], ACT.Copy).then_inc(w1_hi_done, 1)
                elif step == "transpose_x2":
                    act.wait_ge(x2T_ps, g + 1)
                    act.activation(x2T[:, :], W[2][:, 0:T], ACT.Copy).then_inc(x2T_done, 1)
                    act.activation(x2_hi[:, :], W[2][:, 0:T], ACT.Copy).then_inc(x2_hi_done, 1)

            steps = [
                ("keep_v", 1), ("transpose_on", 2, 1), ("hidden", 3, 5), ("hidden", 3, 6), ("feature_maxima", 0),
                ("keep_k", 0), ("hidden", 3, 7), ("transpose_x2", 2), ("landmarks", 0), ("send_maxima", 1),
                ("first_part", 0, 0), ("key_products", 0), ("hidden", 2, 0), ("combine_products", 0), ("weigh", 2),
                ("attend", 1, 0), ("hidden", 2, 1), ("other_parts", 0, 0), ("attend", 1, 1), ("attend", 1, 2),
                ("transpose_gates", 2), ("transpose_x1", 0), ("attend", 1, 3), ("hidden", 2, 2), ("attend", 1, 4),
                ("hidden", 2, 3), ("first_part", 0, 1), ("attend", 1, 5), ("collect", 1, 0), ("other_parts", 0, 1),
                ("attend", 1, 6), ("attend", 1, 7), ("hidden", 2, 4), ("transpose_on", 1, 0), ("collect", 1, 1),
            ]
            pipeline(act, steps, do)

        @block.tensor
        def _(pe):
            mm = nc.tensor.matmul

            def do(step, g, par, *more):
                first = isinstance(g, int) and g == 0
                if step == "gate_logits":
                    pe.wait_ge(x2T_done, g + 1)
                    wait(pe, acc_done, GB * E * g)
                    for b in range(GB):
                        last = mm(YB[:, b * P:b * P + P], x2T[:, b * S:b * S + S], gate_s[:, :], start=True, stop=True)
                    last.then_inc(lg_ps, 1)
                elif step == "hidden":
                    e = more[0]
                    if e == 0:
                        pe.wait_ge(x2_hi_done, g + 1)
                        pe.wait_ge(x2_lo_done, g + 1)
                    if e >= 2:
                        pe.wait_ge(h_done, NHB * (E * g + e - 1))
                    for n in range(NHB):
                        block_n = slice(n * P, n * P + P)
                        for w, v in ((w1_lo, x2_hi), (w1_hi, x2_lo), (w1_hi, x2_hi)):
                            last = mm(HB[e % 2][:, n * T:n * T + T], w[:, e, block_n], v[:, :], start=(w is w1_lo), stop=(w is w1_hi and v is x2_hi))
                    last.then_inc(h_ps, 1)
                elif step == "expert_out":
                    e = more[0]
                    pe.wait_ge(h_done, NHB * (E * g + e + 1))
                    if e == 0:
                        pe.wait_ge(lg_done, g + 1)
                    elif more[1:] == (1,):
                        pe.wait_ge(acc_done, GB * (E * g + e) + 1)
                    else:
                        pe.wait_ge(acc_done, GB * (E * g + e))
                    for b in more[1:] or range(GB):
                        for n in range(NHB):
                            last = mm(YB[:, b * D:b * D + D], hs[:, e % 2, n, b * S:b * S + S], w2_s[:, e, n, :],
                                      start=(n == 0), stop=(n == NHB - 1))
                    last.then_inc(ye_ps, 1)
                elif step == "project":
                    pe.wait_ge(xT_in, 16 * (g + 1))
                    if first:
                        pe.wait_ge(attn_w_in, 16)
                    wait(pe, rest_done, 2 * g)
                    for b in range(GB):
                        if b == 1:
                            wait(pe, r2_done, GB * (g - 1))
                        mm(W[4 - b][:, 0:3 * D], xT_s[:, b * S:b * S + S], wqkv_s[:, :], start=True, stop=True).then_inc(qkv_ps, 1)
                elif step == "score_maxima":
                    if more[0] == 0:
                        pe.wait_ge(k_in, 16 * TERMS * (g + 1))
                        pe.wait_ge(q_zb_done, 2 * (g + 1))
                        if first:
                            pe.wait_ge(const_step, 14)
                        pe.wait_ge(vaug_done, g + 1)
                        wait(pe, exp_done, UNITS * g)
                    for u in more:
                        b, quad = u // QUADS, u % QUADS
                        if u >= 2:
                            pe.wait_ge(nm_done, UNITS * g + u - 1)
                        mm(W[u % 2][:, :], ident_b[:, :], mask4[:, :, :], start=True, stop=False, skip_group_check=True)
                        for c in range(4):
                            h = 4 * quad + c
                            last = mm(W[u % 2][:, c * S:c * S + S], q_zb[:, h % 2, h // 2, b, :], k_dn[:, par, h // 2, b, :],
                                      start=False, stop=(c == 3), skip_group_check=True)
                        last.then_inc(s_ps, 1)
                elif step == "transpose_gates":
                    pe.wait_ge(gates_done, g + 1)
                    if isinstance(g, int) and g + 1 >= NG:
                        pe.wait_ge(r2_done, GB * (g + 1))
                    else:
                        pe.wait_ge(mT_done, g + 2)
                    for b in range(GB):
                        last = nc.tensor.transpose(W[3][:, b * S:b * S + S], gates[:, b, :], ident[:, :])
                    last.then_inc(gT_ps, 1)
                elif step == "gate_bias":
                    pe.wait_ge(gT_done, g + 1)
                    for b in range(GB):
                        last = mm(W[3][:, T + b * D:T + b * D + D], gT[:, b, :], b2_s[:, :], start=True, stop=True)
                    last.then_inc(b2_ps, 1)
                elif step == "landmarks":
                    if first:
                        pe.wait_ge(consts_ready, 1)
                    pe.wait_ge(e_done, 2 * GB * (g + 1))
                    wait(pe, nm_done, UNITS * g)
                    for b in range(GB):
                        last = nc.tensor.transpose(W[0][:, b * S:b * S + S], eqk[:, b, 0, :], ident[:, :])
                    last.then_inc(eqT_ps, 1)
                    pe.wait_ge(kn_done, GB * (g + 1))
                    mm(W[1][:, 0:T], pairs[:, :], kn[:, :, :], start=True, stop=True).then_inc(mk_ps, 1)
                elif step == "send_maxima":
                    pe.wait_ge(nm_step, 4 * (g + 1))
                    if isinstance(g, int) and g + 1 >= NG:
                        pe.wait_ge(r2_done, GB * g)
                    else:
                        pe.wait_ge(qkv_done, GB * (g + 2))
                    nc.tensor.transpose(W[3][0:2 * 3 * NMR, 0:S // 2].bitcast(BF16), nm_p[:, :, :, :].rearrange("p n k r -> p (n k r)"),
                                        ident_b[:, :]).then_inc(mT_ps, 1)
                elif step == "key_products":
                    pe.wait_ge(mk_done, g + 1)
                    pe.wait_ge(eqT_done, g + 1)
                    pe.wait_ge(kv_done, GB * (g + 1))
                    for b in range(GB):
                        last = mm(W[0][:, b * 2 * D:(b + 1) * 2 * D], kn[:, b, :], mkkv[:, b, :, :], start=True, stop=True)
                    last.then_inc(gh_ps, 1)
                elif step == "combine_products":
                    pe.wait_ge(gh_done, g + 1)
                    for b in range(GB):
                        last = mm(W[1][:, b * D:b * D + D], gh[:, b, 0, :], gh[:, b, 1, :], start=True, stop=True)
                    last.then_inc(r_ps, 1)
                elif step == "self_output":
                    pe.wait_ge(r_done, g + 1)
                    wait(pe, x2_hi_done, g - 1)
                    wait(pe, x2T_done, g - 1)
                    for b in range(GB):
                        last = mm(W[2][:, b * D:b * D + D], eqT[:, b * S:b * S + S], r_s[:, b, :], start=True, stop=True)
                    last.then_inc(attn_ps, 1)
                elif step == "project_k":
                    pe.wait_ge(cT_in, 16 * (g + 1))
                    pe.wait_ge(qkv_done, GB * (g + 1))
                    if first:
                        pe.wait_ge(xattn_w_in, 64)
                    mm(W[4][:, 0:T], xwk_s[:, :], cT_s[:, :], start=True, stop=True).then_inc(kq_ps, 1)
                elif step == "transpose_x1":
                    pe.wait_ge(rest_done, 2 * g + 1)
                    pe.wait_ge(x1_done, GB * (g + 1))
                    for b in range(GB):
                        last = nc.tensor.transpose(W[4][:, b * S:b * S + S], x1[:, par, b, :], ident[:, :])
                    last.then_inc(x1T_ps, 1)
                elif step == "project_q":
                    pe.wait_ge(x1T_done, g + 1)
                    mm(W[4][:, T:2 * T], xwq_s[:, :], x1T[:, :], start=True, stop=True).then_inc(kq_ps, 1)
                elif step == "attend":
                    if more[0] == 0:
                        pe.wait_ge(m_in, 16 * 2 * (g + 1))
                        if not (isinstance(g, int) and g + 1 >= NG):
                            pe.wait_ge(gh_done, g + 2)
                            pe.wait_ge(r_done, g + 2)
                    if more[0] == LAG:
                        wait(pe, x2_hi_done, g)
                        wait(pe, x2T_done, g)
                    if more[0] == LAG + QUADS:
                        wait(pe, bias_done, g)
                    if more[0] == LAG and not (isinstance(g, int) and g + 1 >= NG):
                        pe.wait_ge(r1_done, GB * (g + 2))
                    for u in more:
                        if u < UNITS:
                            b, quad = u // QUADS, u % QUADS
                            if u >= 2:
                                pe.wait_ge(exp_done, UNITS * g + u - 1)
                            for j in range(2):
                                pair = 2 * quad + j
                                last = mm(W[u % 2][:, j * 2 * S:(j + 1) * 2 * S], k_dn[:, par, pair, b, :], q_zb[:, :, pair, b, :],
                                          start=True, stop=True)
                            last.then_inc(st_ps, 1)
                        if u >= LAG:
                            v = u - LAG
                            b, quad = v // QUADS, v % QUADS
                            pe.wait_ge(sel_done, UNITS * g + v + 1)
                            for c in range(4):
                                last = mm(W[2 + b][K_OUT * c:K_OUT * c + K_OUT, quad * S:quad * S + S],
                                          vaug[:, b, 4 * quad + c, :], at[:, v % 3, c, :], start=True, stop=True,
                                          tile_position=(0, K_OUT * c))
                            last.then_inc(av_ps, 1)
                elif step == "project_v":
                    wait(pe, exp_done, UNITS * g)
                    for b in range(GB):
                        last = mm(W[0][:, b * D:b * D + D], cT_s[:, b * S:b * S + S], xwv_s[:, :], start=True, stop=True)
                    last.then_inc(v_ps, 1)
                elif step == "normalise":
                    for b in more:
                        pe.wait_ge(oT_done, GB * g + b + 1)
                        for c in range(QUADS):
                            last = nc.tensor.transpose(W[2 + b][:, c * P:c * P + P], oT[:, b, c, :], ident[:, :])
                        last.then_inc(oo_ps, 1)
                elif step == "transpose_on":
                    for b in more:
                        pe.wait_ge(on_done, GB * g + b + 1)
                        nc.tensor.transpose(W[2 + b][:, 0:S], on[:, b, :], ident[:, :]).then_inc(onT_ps, 1)
                elif step == "cross_output":
                    for b in more:
                        pe.wait_ge(onT_done, GB * g + b + 1)
                        mm(W[2 + b][:, D:2 * D], onT[:, b, :], xwo_s[:, :], start=True, stop=True).then_inc(y_ps, 1)
                elif step == "transpose_x2":
                    pe.wait_ge(x2_done, GB * (g + 1))
                    if first:
                        pe.wait_ge(expert_w_in, 16 * 5)
                        pe.wait_ge(w1_lo_done, 1)
                    for b in range(GB):
                        last = nc.tensor.transpose(W[2][:, b * S:b * S + S], x2[:, b, :], ident[:, :])
                    last.then_inc(x2T_ps, 1)

            steps = [
                ("cross_output", 2, 0), ("normalise", 2, 1), ("expert_out", 3, 3, 1), ("hidden", 3, 5),
                ("transpose_on", 2, 1), ("expert_out", 3, 4), ("cross_output", 2, 1), ("project", 0), ("score_maxima", 1, 0),
                ("score_maxima", 1, 1), ("hidden", 3, 6), ("score_maxima", 1, 2), ("score_maxima", 1, 3),
                ("expert_out", 3, 5), ("hidden", 3, 7), ("score_maxima", 1, 4), ("score_maxima", 1, 5), ("expert_out", 3, 6),
                ("score_maxima", 1, 6), ("score_maxima", 1, 7), ("transpose_x2", 2), ("expert_out", 3, 7), ("landmarks", 0),
                ("project_k", 0), ("send_maxima", 1), ("key_products", 0), ("hidden", 2, 0), ("gate_logits", 2),
                ("combine_products", 0), ("hidden", 2, 1), ("attend", 1, 0), ("self_output", 0), ("attend", 1, 1),
                ("expert_out", 2, 0), ("transpose_gates", 2), ("attend", 1, 2), ("hidden", 2, 2), ("gate_bias", 2),
                ("attend", 1, 3), ("transpose_x1", 0), ("expert_out", 2, 1), ("attend", 1, 4), ("hidden", 2, 3),
                ("project_q", 0), ("attend", 1, 5), ("expert_out", 2, 2), ("attend", 1, 6), ("normalise", 1, 0),
                ("attend", 1, 7), ("hidden", 2, 4), ("project_v", 0), ("attend", 1, 8), ("transpose_on", 1, 0),
                ("attend", 1, 9), ("expert_out", 2, 3, 0),
            ]
            pipeline(pe, steps, do)

        @block.vector
        def _(dve):
            fills = [(gate_s, 0.0), (b2_s, 0.0), (gates, 0.0), (two, LOWEST), (lg, LOWEST), (nm_p, 0.0)]
            for tile, value in fills:
                dve.memset(tile[tuple(slice(None) for _ in tile.shape)], value).then_inc(dve_set, 1)

            def moments(g, n, src):
                for b in range(GB):
                    last = dve.bn_stats(stats[n][:, b, :], src[:, b, :])
                last.then_inc(stats_done[n], 1)
                hold(dve, stats_done[n], g + 1)
                for b in range(GB):
                    last = dve.bn_aggr(mv[n][:, b, :], stats[n][:, b, :])
                last.then_inc(mv_done[n], 1)

            def norm(g, n, src, dst, done):
                dve.wait_ge(rstd_done[n], g + 1)
                for b in range(GB):
                    dve.tensor_scalar(dst[:, b, :], src[:, b, :], mv[n][:, b, 0:1], rstd[n][:, b:b + 1], ALU.subtract, ALU.mult).then_inc(done, 1)

            def do(step, g, par, *more):
                if step == "gate_logits":
                    dve.wait_ge(lg_ps, g + 1)
                    dve.tensor_tensor(lg[:, :, 0:E], YB[:, 0:T].rearrange("p (b e) -> p b e", b=GB)[:, :, 0:E],
                                      gateb_s[:, :].unsqueeze(1).broadcast_to([P, GB, E]), ALU.add).then_inc(lg_done, 1)
                    hold(dve, lg_done, g + 1)
                    for b in range(GB):
                        dve.max(top[:, b, :], lg[:, b, 0:E]).then_inc(top_step, 1)
                    dve.wait_ge(top_step, 7 * g + 2)
                    dve.tensor_copy(two[:, :, 0:2], top[:, :, 0:2]).then_inc(top_step, 1)
                    dve.tensor_tensor(lsh[:, :, :], lg[:, :, 0:E], top[:, :, 0:1].broadcast_to([P, GB, E]), ALU.subtract).then_inc(top_step, 1)
                elif step == "top_two":
                    hold(dve, top_step, 7 * g + 4)
                    for b in range(GB):
                        dve.match_replace(rep[:, b, :], two[:, b, :], lg[:, b, :], LOWEST).then_inc(top_step, 1)
                    dve.wait_ge(top_step, 7 * g + 6)
                    dve.tensor_tensor(chosen[:, :, :], lg[:, :, 0:E], rep[:, :, 0:E], ALU.not_equal).then_inc(top_step, 1)
                elif step == "weigh":
                    dve.wait_ge(eg_done, g + 1)
                    dve.reduce_sum(gsum[:, :], eg[:, :, :], AX).then_inc(sum_step, 1)
                    dve.wait_ge(sum_step, 3 * g + 1)
                    dve.reciprocal(grec[:, :], gsum[:, :]).then_inc(sum_step, 1)
                    dve.wait_ge(top_step, 7 * g + 7)
                    dve.tensor_tensor(gmul[:, :, :], eg[:, :, :], chosen[:, :, :], ALU.mult).then_inc(sum_step, 1)
                elif step == "gates":
                    dve.wait_ge(sum_step, 3 * g + 3)
                    dve.tensor_tensor(gates[:, :, 0:E], gmul[:, :, :], grec[:, :].unsqueeze(2).broadcast_to([P, GB, E]), ALU.mult).then_inc(gates_done, 1)
                elif step == "add_bias":
                    dve.wait_ge(b2_ps, g + 1)
                    dve.wait_ge(acc_done, GB * (E * g + 2))
                    dve.tensor_tensor(acc[:, par, :, :], W[3][:, T:2 * T].rearrange("p (b d) -> p b d", b=GB), acc[:, par, :, :], ALU.add).then_inc(bias_done, 1)
                elif step == "gather":
                    e = more[0]
                    dve.wait_ge(ye_ps, OUTS * g + OUT_BY[e] + (more[1] if more[1:] else 0) + 1)
                    for b in more[1:] or range(GB):
                        if e == 0:
                            dve.wait_ge(gates_done, g + 1)
                        elif e == 2:
                            dve.wait_ge(bias_done, g + 1)
                        else:
                            dve.wait_ge(acc_done, GB * (E * g + e - 1) + b + 1)
                        dve.scalar_tensor_tensor(acc[:, par, b, :], YB[:, b * D:b * D + D], gates[:, b, e:e + 1], (acc[:, par, b, :] if e else x2[:, b, :]),
                                                 ALU.mult, ALU.add).then_inc(acc_done, 1)
                elif step == "norm_x1":
                    norm(g, 0, r1, x1[:, par, :, :], x1_done)
                elif step == "moments_x2":
                    dve.wait_ge(r2_done, GB * (g + 1))
                    moments(g, 1, r2)
                elif step == "norm_x2":
                    norm(g, 1, r2, x2, x2_done)
                elif step == "moments_out":
                    dve.wait_ge(acc_done, GB * E * (g + 1))
                    moments(g, 2, acc[:, par, :, :])
                elif step == "norm_out":
                    dve.wait_ge(gateb_in_stores, 16 * (g + 1))
                    norm(g, 2, acc[:, par, :, :], o_s, o_done)
                elif step == "add_biases":
                    if isinstance(g, int) and g == 0:
                        dve.wait_ge(bias_in, 16)
                    wait(dve, e_done, 2 * GB * g)
                    for b in range(GB):
                        dve.wait_ge(qkv_ps, GB * g + b + 1)
                        dve.tensor_tensor(qkv[:, b, :], W[4 - b][:, 0:3 * D], bias_bc[:, :], ALU.add).then_inc(qkv_done, 1)
                elif step == "feature_maxima":
                    for b in range(GB):
                        dve.wait_ge(qkv_done, GB * g + b + 1)
                        dve.tensor_reduce(nmax1[:, b, :], qkv[:, b, 0:2 * D].rearrange("p (n d) -> p n d", n=2), AX, ALU.max,
                                          negate=True).then_inc(nmax_done, 1)
                    if isinstance(g, int) and g == 0:
                        dve.wait_ge(const_step, 13)
                        dve.reduce_sum(parity[:, 0:1], par_tmp[:, :], AX).then_inc(dve_set, 1)
                        dve.wait_ge(dve_set, N_FILLS + 1)
                        dve.tensor_scalar(parity[:, 1:2], parity[:, 0:1], -1.0, 1.0, ALU.mult, ALU.add).then_inc(consts_ready, 1)
                elif step == "spread_q":
                    dve.wait_ge(q_in, 16 * TERMS * (g + 1))
                    wait(dve, st_ps, UNITS * g)
                    for n in more:
                        dve.tensor_scalar(q_zb[:, n, :, :, :], q_dn[:, :, :, :], parity[:, n:n + 1], None, ALU.mult).then_inc(q_zb_done, 1)
                elif step == "score_maxima":
                    for u in more:
                        b, quad = u // QUADS, u % QUADS
                        dve.wait_ge(s_ps, UNITS * g + u + 1)
                        dve.tensor_reduce(nm[:, :, 2 * quad:2 * quad + 2, b], W[u % 2][:, :].rearrange("p (j r s) -> p r j s", j=2, r=2), AX,
                                          ALU.max, negate=True).then_inc(nm_done, 1)
                elif step == "split_maxima":
                    dve.wait_ge(nm_done, UNITS * (g + 1))
                    wait(dve, mT_ps, g)
                    src = nm[:, :, :, :].rearrange("p n j b -> p n (j b)")
                    res = nm_r[:, :, :, :].rearrange("p n j b -> p n (j b)")
                    dve.tensor_copy(nm_p[:, :, 0, :], src).then_inc(nm_step, 1)
                    dve.wait_ge(nm_step, 4 * g + 1)
                    dve.tensor_tensor(res, src, nm_p[:, :, 0, :], ALU.subtract).then_inc(nm_step, 1)
                    dve.wait_ge(nm_step, 4 * g + 2)
                    dve.tensor_copy(nm_p[:, :, 1, :], res).then_inc(nm_step, 1)
                    dve.wait_ge(nm_step, 4 * g + 3)
                    dve.tensor_tensor(nm_p[:, :, 2, :], res, nm_p[:, :, 1, :], ALU.subtract).then_inc(nm_step, 1)
                elif step == "normalise_k":
                    for b in range(GB):
                        dve.wait_ge(e_done, 2 * GB * g + 2 * b + 2)
                        dve.reciprocal(rs1[:, b, :], sum1[:, b, :]).then_inc(rs1_done, 1)
                elif step == "weigh_values":
                    for b in range(GB):
                        dve.wait_ge(rs1_done, GB * g + b + 1)
                        dve.scalar_tensor_tensor(mkkv[:, b, 1, :], eqk[:, b, 1, :], rs1[:, b, 1:2], qkv[:, b, 2 * D:3 * D],
                                                 ALU.mult, ALU.mult).then_inc(kv_done, 1)
                elif step == "self_output":
                    dve.wait_ge(x_in, 16 * (g + 1))
                    dve.wait_ge(attn_ps, g + 1)
                    for b in range(GB):
                        dve.scalar_tensor_tensor(r1[:, b, :], W[2][:, b * D:b * D + D], rs1[:, b, 0:1], x_s[:, b, :],
                                                 ALU.mult, ALU.add).then_inc(r1_done, 1)
                    dve.wait_ge(r1_done, GB * (g + 1))
                    moments(g, 0, r1)
                elif step == "first_part":
                    q = more[0]
                    dve.wait_ge(p1_done, 2 * g + 1 + q)
                    dve.tensor_tensor(rest[:, q, :], W[4][:, T * q:T * q + T], parts[:, q, 0, :], ALU.subtract).then_inc(rest_done, 1)
                elif step == "other_parts":
                    q = more[0]
                    dve.wait_ge(p2_done, 2 * g + 1 + q)
                    dve.tensor_tensor(parts[:, q, 2, :], rest[:, q, :], parts[:, q, 1, :], ALU.subtract).then_inc(p3_done, 1)
                elif step == "normalise":
                    for b in more:
                        dve.wait_ge(oo_ps, GB * g + b + 1)
                        heads = W[2 + b][:, :].rearrange("p (h k) -> p h k", k=K_OUT)
                        dve.reciprocal(rden[:, b, :], heads[:, :, DH]).then_inc(rden_done, 1)
                        dve.wait_ge(rden_done, GB * g + b + 1)
                        dve.tensor_tensor(on[:, b, :].rearrange("p (h d) -> p h d", h=NH), heads[:, :, 0:DH],
                                          rden[:, b, :].unsqueeze(2).broadcast_to([P, NH, DH]), ALU.mult).then_inc(on_done, 1)
                elif step == "cross_output":
                    for b in more:
                        dve.wait_ge(y_ps, GB * g + b + 1)
                        dve.tensor_tensor(r2[:, b, :], W[2 + b][:, D:2 * D], x1[:, par, b, :], ALU.add).then_inc(r2_done, 1)

            dve.wait_ge(gateb_in_stores, 16)
            steps = [
                ("gather", 3, 4), ("cross_output", 2, 1), ("moments_x2", 2), ("add_biases", 0), ("score_maxima", 1, 0),
                ("score_maxima", 1, 1), ("norm_x2", 2), ("score_maxima", 1, 2), ("feature_maxima", 0),
                ("score_maxima", 1, 3), ("gather", 3, 5), ("score_maxima", 1, 4), ("normalise_k", 0), ("score_maxima", 1, 5),
                ("gather", 3, 6), ("score_maxima", 1, 6), ("score_maxima", 1, 7), ("weigh_values", 0), ("split_maxima", 1),
                ("gather", 3, 7), ("first_part", 0, 0), ("moments_out", 3), ("gate_logits", 2), ("top_two", 2), ("weigh", 2),
                ("gates", 2), ("self_output", 0), ("other_parts", 0, 0), ("gather", 2, 0), ("norm_x1", 0), ("gather", 2, 1),
                ("norm_out", 3), ("add_bias", 2), ("first_part", 0, 1), ("other_parts", 0, 1), ("gather", 2, 2),
                ("normalise", 1, 0), ("gather", 2, 3, 0), ("normalise", 1, 1), ("gather", 2, 3, 1), ("cross_output", 1, 0),
                ("spread_q", 0, 0), ("spread_q", 0, 1),
            ]
            pipeline(dve, steps, do)


_ORDER = ["x", "x_t", "ctx_t", "w_qkv", "b_qkv", "xwq_t", "xwk_t", "xwv_t", "xwo_t", "gate_t", "gate_b", "w1", "b1", "w2", "b2"]


def kernel(**inputs):
    import numpy as _np
    import concourse.bacc as _bacc
    from concourse import mybir as _mybir
    from concourse.bass_utils import run_bass_kernel_spmd as _run

    a = {k: _np.asarray(v) for k, v in inputs.items()}
    nb, s, d = a["x"].shape
    e, hid = a["L0_ffn_b1"].shape
    def by_parity(w):
        return w.T.reshape(d, 8, 2, 8).transpose(0, 2, 3, 1).reshape(d, d)

    laid = {
        "x": a["x"],
        "x_t": a["x"].reshape(nb * s, d).T,
        "ctx_t": a["ctx_1024"].reshape(nb * s, d).T,
        "w_qkv": _np.stack([a["L0_attn_Wq"], a["L0_attn_Wk"], a["L0_attn_Wv"]]),
        "b_qkv": _np.concatenate([a["L0_attn_bq"], a["L0_attn_bk"], a["L0_attn_bv"]]),
        "xwq_t": by_parity(a["L0_xattn_Wq"]),
        "xwk_t": by_parity(a["L0_xattn_Wk"]),
        "xwv_t": a["L0_xattn_Wv"].T,
        "xwo_t": a["L0_xattn_Wo"].T,
        "gate_t": a["L0_ffn_gate_w"].T,
        "gate_b": a["L0_ffn_gate_b"],
        "w1": a["L0_ffn_w1"],
        "b1": a["L0_ffn_b1"].reshape(e, hid // 128, 128).transpose(2, 0, 1),
        "w2": a["L0_ffn_w2"],
        "b2": a["L0_ffn_b2"],
    }
    nc = _bacc.Bacc("TRN2", target_bir_lowering=False, num_devices=1)
    arrays, args = {}, []
    for name in _ORDER:
        v = _np.ascontiguousarray(laid[name])
        arrays[f"in_{name}"] = v
        args.append(nc.dram_tensor(f"in_{name}", v.shape, _mybir.dt.from_np(v.dtype), kind="ExternalInput").ap())
    args.append(nc.dram_tensor("out_0", a["x"].shape, _mybir.dt.float32, kind="ExternalOutput").ap())
    decoder_layer(nc, *args)
    r = _run(nc, [arrays], core_ids=[0])
    return r.results[0]["out_0"]
```
